# Optimizing a Trainium2 kernel written in Bass

```python
import numpy as np
import jax
import jax.numpy as jnp

def _softmax(x, axis=-1):
    return jax.nn.softmax(x, axis=axis)
def _gelu(x):
    return jax.nn.gelu(x, approximate=True)
def _silu(x):
    return jax.nn.silu(x)
def _sigmoid(x):
    return jax.nn.sigmoid(x)
def _layernorm(x, axis=-1, eps=1e-5):
    m = jnp.mean(x, axis=axis, keepdims=True)
    v = jnp.var(x, axis=axis, keepdims=True)
    return (x - m) / jnp.sqrt(v + eps)
def _scatter_add(tgt, idx, src, axis=0):
    return tgt.at[idx].add(src)
def _segment_sum(src, seg, n):
    return jax.ops.segment_sum(src, seg, n)

kernel_name = 'mk_adj_resnorm_d4_adj_512_f62af0'

def setup_inputs(seed: int = 0):
    np.random.seed(seed)
    _w = jnp.asarray
    def _rec_inputs():
        import jax
        import jax.numpy as jnp
        _gk = jax.random.key(seed)
        x = -0.0002928 + 1 * jax.random.normal(jax.random.fold_in(_gk, 1), (128, 64, 512), jnp.float32)
        _a = jax.random.bernoulli(jax.random.fold_in(_gk, 2), 0.0625, (128, 64, 64))
        _a = jnp.logical_or(_a, jnp.swapaxes(_a, -1, -2))
        _a = jnp.logical_or(_a, jnp.eye(64, dtype=bool))
        _af = _a.astype(jnp.float32)
        _af = _af * jax.random.uniform(jax.random.fold_in(_gk, 3), (128, 64, 64), jnp.float32, 0.05, 1)
        adj = _af
        return x, adj
    x, adj = _rec_inputs()
    def _L0_gnn_setup():
        import jax, jax.numpy as jnp
        import numpy as np
        B, N, DIN, DOUT, K = (4, 2048, 512, 512, 3)
        key = jax.random.key(seed)
        ks = jax.random.split(key, 8)
        X = jax.random.normal(ks[0], (B, N, DIN), dtype=jnp.float32)
        A = jax.random.uniform(ks[1], (B, N, N), dtype=jnp.float32)
        Wv = jax.random.normal(ks[2], (DIN, DOUT), dtype=jnp.float32) * 0.02
        bv = jax.random.normal(ks[3], (DOUT,), dtype=jnp.float32) * 0.02
        aw = jax.random.normal(ks[4], (2 * DOUT, 1), dtype=jnp.float32) * 0.05
        ab = jax.random.normal(ks[5], (1,), dtype=jnp.float32) * 0.05
        Wk = jax.random.normal(ks[6], (K, DIN, DOUT), dtype=jnp.float32) * 0.02
        bk = jax.random.normal(ks[7], (K, DOUT), dtype=jnp.float32) * 0.02
        return {'X': X, 'A': A, 'Wv': Wv, 'bv': bv, 'aw': aw, 'ab': ab, 'Wk': Wk, 'bk': bk}
    _L0_gnn_all = _L0_gnn_setup()
    _L0_gnn_in = {k: v for k, v in _L0_gnn_all.items() if k in ('Wv', 'bv', 'aw', 'ab', 'Wk', 'bk', )}
    del _L0_gnn_all

    def _L1_gnn_setup():
        import jax, jax.numpy as jnp
        import numpy as np
        B, N, F_IN, F_HID, F_OUT = (32, 1024, 512, 512, 512)

        def _gcn_layer(x, adj, W, b):
            support = jnp.einsum('bnf,fh->bnh', x, W)
            return jnp.einsum('bnm,bmh->bnh', adj, support) + b
        key = jax.random.key(seed)
        ks = jax.random.split(key, 8)

        def xavier(k, fan_in, fan_out):
            bound = float(np.sqrt(6.0 / (fan_in + fan_out)))
            return jax.random.uniform(k, (fan_in, fan_out), jnp.float32, -bound, bound)
        return {'batch_graph': jax.random.normal(ks[0], (B, N, F_IN), jnp.float32), 'adj': jax.random.uniform(ks[1], (B, N, N), jnp.float32), 'W1': xavier(ks[2], F_IN, F_HID), 'b1': jnp.zeros((F_HID,), jnp.float32), 'W2': xavier(ks[3], F_HID, F_HID), 'b2': jnp.zeros((F_HID,), jnp.float32), 'W3': xavier(ks[4], F_HID, F_OUT), 'b3': jnp.zeros((F_OUT,), jnp.float32)}
    _L1_gnn_all = _L1_gnn_setup()
    _L1_gnn_in = {k: v for k, v in _L1_gnn_all.items() if k in ('W1', 'b1', 'W2', 'b2', 'W3', 'b3', )}
    del _L1_gnn_all

    def _L2_gnn_setup():
        import jax, jax.numpy as jnp
        import numpy as np
        B, N, D = (8, 2048, 512)
        key = jax.random.key(seed)
        ks = jax.random.split(key, 8)
        scale = 0.5 / np.sqrt(D)
        x = jax.random.normal(ks[0], (B, N, D), dtype=jnp.float32)
        adj = jax.random.uniform(ks[1], (B, N, N), dtype=jnp.float32)
        Wq_w = jax.random.normal(ks[2], (D, D), dtype=jnp.float32) * scale
        Wk_w = jax.random.normal(ks[3], (D, D), dtype=jnp.float32) * scale
        Wv_w = jax.random.normal(ks[4], (D, D), dtype=jnp.float32) * scale
        Wq_b = jnp.zeros((D,), dtype=jnp.float32)
        Wk_b = jnp.zeros((D,), dtype=jnp.float32)
        Wv_b = jnp.zeros((D,), dtype=jnp.float32)
        return {'x': x, 'adj': adj, 'Wq_w': Wq_w, 'Wq_b': Wq_b, 'Wk_w': Wk_w, 'Wk_b': Wk_b, 'Wv_w': Wv_w, 'Wv_b': Wv_b}
    _L2_gnn_all = _L2_gnn_setup()
    _L2_gnn_in = {k: v for k, v in _L2_gnn_all.items() if k in ('Wq_w', 'Wq_b', 'Wk_w', 'Wk_b', 'Wv_w', 'Wv_b', )}
    del _L2_gnn_all

    def _L3_gnn_setup():
        import jax, jax.numpy as jnp
        import numpy as np
        IN_DIM = 512
        ATT_DIM = 64
        B, N = (4, 4096)
        key = jax.random.key(seed)
        k1, k2, k3, k4 = jax.random.split(key, 4)
        x = jax.random.normal(k1, (B, N, IN_DIM), dtype=jnp.float32)
        adj_matrix = (jax.random.uniform(k2, (B, N, N)) < 0.05).astype(jnp.float32)
        W_qk = jax.random.normal(k3, (2 * ATT_DIM, IN_DIM), dtype=jnp.float32) / np.sqrt(IN_DIM)
        W_v = jax.random.normal(k4, (IN_DIM, IN_DIM), dtype=jnp.float32) / np.sqrt(IN_DIM)
        return {'x': x, 'adj_matrix': adj_matrix, 'W_qk': W_qk, 'W_v': W_v}
    _L3_gnn_all = _L3_gnn_setup()
    _L3_gnn_in = {k: v for k, v in _L3_gnn_all.items() if k in ('W_qk', 'W_v', )}
    del _L3_gnn_all

    return {
        "x": x,
        "adj": adj,
        "L0_gnn_Wv": _L0_gnn_in["Wv"],
        "L0_gnn_bv": _L0_gnn_in["bv"],
        "L0_gnn_aw": _L0_gnn_in["aw"],
        "L0_gnn_ab": _L0_gnn_in["ab"],
        "L0_gnn_Wk": _L0_gnn_in["Wk"],
        "L0_gnn_bk": _L0_gnn_in["bk"],
        "L1_gnn_W1": _L1_gnn_in["W1"],
        "L1_gnn_b1": _L1_gnn_in["b1"],
        "L1_gnn_W2": _L1_gnn_in["W2"],
        "L1_gnn_b2": _L1_gnn_in["b2"],
        "L1_gnn_W3": _L1_gnn_in["W3"],
        "L1_gnn_b3": _L1_gnn_in["b3"],
        "L2_gnn_Wq_w": _L2_gnn_in["Wq_w"],
        "L2_gnn_Wq_b": _L2_gnn_in["Wq_b"],
        "L2_gnn_Wk_w": _L2_gnn_in["Wk_w"],
        "L2_gnn_Wk_b": _L2_gnn_in["Wk_b"],
        "L2_gnn_Wv_w": _L2_gnn_in["Wv_w"],
        "L2_gnn_Wv_b": _L2_gnn_in["Wv_b"],
        "L3_gnn_W_qk": _L3_gnn_in["W_qk"],
        "L3_gnn_W_v": _L3_gnn_in["W_v"],
    }

def reference(x, adj, L0_gnn_Wv, L0_gnn_bv, L0_gnn_aw, L0_gnn_ab, L0_gnn_Wk, L0_gnn_bk, L1_gnn_W1, L1_gnn_b1, L1_gnn_W2, L1_gnn_b2, L1_gnn_W3, L1_gnn_b3, L2_gnn_Wq_w, L2_gnn_Wq_b, L2_gnn_Wk_w, L2_gnn_Wk_b, L2_gnn_Wv_w, L2_gnn_Wv_b, L3_gnn_W_qk, L3_gnn_W_v):
    import jax
    import jax.numpy as jnp
    def _L0_gnn_ref(X, A, Wv, bv, aw, ab, Wk, bk):
        import jax, jax.numpy as jnp
        import numpy as np
        B, N, DIN, DOUT, K = (4, 2048, 512, 512, 3)
        d = Wv.shape[1]
        Xw = X @ Wv + bv
        sj = Xw @ aw[:d, 0]
        si = Xw @ aw[d:, 0]
        e = jax.nn.leaky_relu(sj[:, None, :] + si[:, :, None] + ab[0], negative_slope=0.2)
        alpha_matrix = A * jnp.exp(e)
        transition = alpha_matrix / (jnp.sum(alpha_matrix, axis=-1, keepdims=True) + 1e-12)
        H = jnp.zeros(X.shape[:-1] + (d,), dtype=X.dtype)
        Xk = X
        for k in range(Wk.shape[0]):
            H = H + Xk @ Wk[k] + bk[k]
            Xk = jnp.einsum('bij,bjd->bid', transition, Xk)
        return jax.nn.relu(H)

    def _L1_gnn_ref(batch_graph, adj, W1, b1, W2, b2, W3, b3):
        import jax, jax.numpy as jnp
        import numpy as np
        B, N, F_IN, F_HID, F_OUT = (32, 1024, 512, 512, 512)

        def _gcn_layer(x, adj, W, b):
            support = jnp.einsum('bnf,fh->bnh', x, W)
            return jnp.einsum('bnm,bmh->bnh', adj, support) + b
        x = jax.nn.relu(_gcn_layer(batch_graph, adj, W1, b1))
        x = jax.nn.relu(_gcn_layer(x, adj, W2, b2))
        out = _gcn_layer(x, adj, W3, b3)
        return out

    def _L2_gnn_ref(x, adj, Wq_w, Wq_b, Wk_w, Wk_b, Wv_w, Wv_b):
        import jax, jax.numpy as jnp
        import numpy as np
        B, N, D = (8, 2048, 512)
        query = jnp.einsum('bnd,od->bno', x, Wq_w) + Wq_b
        keyt = jnp.einsum('bnd,od->bno', x, Wk_w) + Wk_b
        value = jnp.einsum('bnd,od->bno', x, Wv_w) + Wv_b
        weight = jnp.einsum('bqd,bkd->bqk', query, keyt)
        weight = adj * jnp.exp(weight)
        weight = weight / jnp.sum(weight, axis=2, keepdims=True)
        return jnp.einsum('bqk,bkd->bqd', weight, value)

    def _L3_gnn_ref(x, adj_matrix, W_qk, W_v):
        import jax, jax.numpy as jnp
        import numpy as np
        IN_DIM = 512
        ATT_DIM = 64
        B, N = (4, 4096)
        qk = jnp.einsum('bnd,ed->bne', x, W_qk)
        q, k = jnp.split(qk, 2, axis=-1)
        v = jnp.einsum('bnd,ed->bne', x, W_v)
        inv_scale = 1.0 / ATT_DIM ** 0.5
        scores = jnp.einsum('bnd,bmd->bnm', q, k) * inv_scale
        w = jnp.sum(scores * adj_matrix, axis=-1, keepdims=True)
        w = jax.nn.softmax(w, axis=1)
        return w * v

    x = _layernorm(x + _L0_gnn_ref(x, adj, L0_gnn_Wv, L0_gnn_bv, L0_gnn_aw, L0_gnn_ab, L0_gnn_Wk, L0_gnn_bk), axis=-1)
    x = _layernorm(x + _L1_gnn_ref(x, adj, L1_gnn_W1, L1_gnn_b1, L1_gnn_W2, L1_gnn_b2, L1_gnn_W3, L1_gnn_b3), axis=-1)
    x = _layernorm(x + _L2_gnn_ref(x, adj, L2_gnn_Wq_w, L2_gnn_Wq_b, L2_gnn_Wk_w, L2_gnn_Wk_b, L2_gnn_Wv_w, L2_gnn_Wv_b), axis=-1)
    x = _layernorm(x + _L3_gnn_ref(x, adj, L3_gnn_W_qk, L3_gnn_W_v), axis=-1)
    return x


_drawn_inputs = setup_inputs


def setup_inputs(seed=0):
    import zlib

    import numpy as np

    out = dict(_drawn_inputs(seed))
    spreads = {'L1_gnn_b1': (0.0, 0.1),
     'L1_gnn_b2': (0.0, 0.324),
     'L1_gnn_b3': (0.0, 0.709),
     'L2_gnn_Wq_b': (0.0, 0.536),
     'L2_gnn_Wk_b': (0.0, 2.0),
     'L2_gnn_Wv_b': (0.0, 0.1)}
    factors = {'L0_gnn_bv': 33.664}
    for name, (base, spread) in spreads.items():
        noise = np.random.default_rng([zlib.crc32(name.encode()), seed]).standard_normal(out[name].shape)
        drawn = base * np.exp(spread * noise) if base else spread * noise
        out[name] = jnp.asarray(drawn.astype(out[name].dtype))
    for name, factor in factors.items():
        out[name] = (out[name] * factor).astype(out[name].dtype)
    return out
```

```python
from contextlib import ExitStack

import concourse.bass as bass
from concourse import mybir

F32 = mybir.dt.float32
F32R = mybir.dt.float32r
ALU = mybir.AluOpType
ACT = mybir.ActivationFunctionType
AX = mybir.AxisListType

H, L = 0, 1
PASSES = ((H, H), (H, L), (L, H))
P = 128
LAYERS = 4
LN_EPS = 1e-5
ROWSUM_EPS = 1e-12
SLOPE = 0.2


def wait(eng, sem, count):
    if isinstance(count, int) and count <= 0:
        return
    eng.wait_ge(sem, count)


def build(nc, x, adj, Wv0, bv0, aw0, ab0, Wk0, bk0, W1, b1, W2, b2, W3, b3,
          Wq2, bq2, Wk2, bk2, Wv2, bv2, Wqk3, Wv3, out):
    graphs, N, D = x.shape
    C = D // P
    PAIRS = graphs * N // P
    E3 = Wqk3.shape[0] // 2
    SCALE3 = float(E3) ** -0.5
    HALVES = (slice(0, N), slice(N, P))
    assert 2 * N == P and D == 512 and 2 * E3 == P and PAIRS > 2 * LAYERS - 2

    x_pairs = x.rearrange("(t g) n d -> t (g n) d", g=2)
    out_pairs = out.rearrange("(t g) n d -> t (g n) d", g=2)
    adj_pairs = adj.rearrange("(t g) i j -> t (g i) j", g=2)
    adj_graphs = adj.rearrange("(t g) i j -> t g i j", g=2)

    with ExitStack() as ctx:
        def sb(name, shape, dt=F32):
            return ctx.enter_context(nc.sbuf_tensor(name, shape, dt))

        def sem(name):
            return ctx.enter_context(nc.semaphore(name))

        plain = [sb(f"w_{n}", [P, 2, C, D], F32R)
                 for n in ("hop1", "hop2", "hop0", "gcn1", "gcn2", "gcn3")]
        w_hop1, w_hop2, w_hop0, w_gcn1, w_gcn2, w_gcn3 = plain
        w_qk2 = sb("w_qk2", [P, 2, C, D], F32R)
        w_v2 = sb("w_v2", [P, 2, C, D], F32R)
        w_v3 = sb("w_v3", [P, 2, C, D], F32R)
        w_qk3 = sb("w_qk3", [P, 2, C, 2 * E3], F32R)
        w_edge = sb("w_edge", [P, 2, C, 2], F32R)
        w_row2 = sb("w_row2", [P, 2, C, 2], F32R)
        ident = sb("ident", [P, P])
        same_graph = sb("same_graph", [P, P])
        node_ident = sb("node_ident", [P, N])
        bias_rows = sb("bias_rows", [P, D], F32R)
        BIAS_ROWS = {"hop": (0, 6), "gcn1": (6, 8), "gcn2": (8, 10), "gcn3": (10, 12),
                     "v2": (12, 14), "key2": (14, 16)}
        select = {n: sb(f"select_{n}", [P, P], F32R) for n in BIAS_ROWS}
        cols = sb("cols", [P, 96])
        used_cols = [0]

        def col(n=1):
            used_cols[0] += n
            return cols[:, used_cols[0] - n:used_cols[0]]

        edge_const = col()
        row_const = col()
        even, odd = col(), col()
        minus_half = col()

        SLOTS = 5
        with ExitStack() as staging:
            def stage(name, shape, dt=F32):
                return staging.enter_context(nc.sbuf_tensor(name, shape, dt))

            raw = [stage(f"raw{i}", [P, C, D]) for i in range(SLOTS)]
            aw_all = stage("aw_all", [P, 2, D])
            bv_all = stage("bv_all", [P, D])
            bias_raw = stage("bias_raw", [P, D])
            bias_high = stage("bias_high", [P, D], F32R)
            ones = stage("ones", [P, P])
            bq_col = stage("bq_col", [P, C])
            bk_col = stage("bk_col", [P, C])
            bq_wide = stage("bq_wide", [P, C, 16])
            edge_raw = stage("edge_raw", [P, C, 2])
            row_raw = stage("row_raw", [P, C, 2])
            ab_all = stage("ab_all", [P, 1])
            pick = stage("pick", [P, len(BIAS_ROWS)])
            junk = stage("junk", [P, D])
            sums = stage("sums", [P, 3])

        x0_in = sb("x0_in", [P, D])
        x0_res = sb("x0_res", [P, D])
        x0T = sb("x0T", [P, 2, C, P], F32R)
        hop_y = sb("hop_y", [P, 2, D], F32R)
        adj0 = sb("adj0", [P, N])
        edge0 = sb("edge0", [P, N])
        diag0 = sb("diag0", [P, N])
        trans0 = sb("trans0", [P, P])
        trans0T = sb("trans0T", [P, 2, P], F32R)
        x1 = sb("x1", [P, D])
        node1 = sb("node1", [P, 2, D], F32R)
        feat1 = sb("feat1", [P, 2, C, P], F32R)
        adj_blocks = sb("adj_blocks", [P, 2, P])
        adjT = sb("adjT", [P, 2, 2, P], F32R)
        x2 = sb("x2", [P, D])
        x2T = sb("x2T", [P, 2, C, P], F32R)
        query2T = sb("query2T", [P, 2, C, P], F32R)
        value2 = sb("value2", [P, 2, D], F32R)
        adj2 = sb("adj2", [P, N])
        attn2 = sb("attn2", [P, N])
        probs2 = sb("probs2", [P, P])
        probs2T = sb("probs2T", [P, 2, P], F32R)
        x3 = sb("x3", [P, D])
        x3T = sb("x3T", [P, 2, C, P], F32R)
        q3 = sb("q3", [P, E3])
        k3 = sb("k3", [P, 2, E3], F32R)
        work3 = sb("work3", [P, N])
        diag3 = sb("diag3", [P, N])
        x4 = sb("x4", [P, D])
        xs = [None, x1, x2, x3, x4]
        edge_i = col()
        rowsum0, inv0 = col(), col()
        rowbias2 = col()
        rowsum2, inv2 = col(), col()
        w3, max3, exp3, sum3, inv3, gate3 = col(), col(), col(), col(), col(), col()
        stats = [col(6) for _ in range(LAYERS)]
        moments = [col(2) for _ in range(LAYERS)]
        var_eps = [col() for _ in range(LAYERS)]
        rstd = [col() for _ in range(LAYERS)]

        SETUP_GROUPS = C + 3 + 2 * C + 1

        bank = [ctx.enter_context(nc.psum_tensor(f"bank{i}", [P, D], F32)) for i in range(8)]
        HOP0, HOP1, TURN, FEAT1, NODE1, MID2, WIDE, SMALL = range(8)

        s_slot = [sem(f"slot{i}") for i in range(SLOTS)]
        s_vec_loaded = sem("vec_loaded")
        s_pool_const = sem("pool_const")
        s_dve_setup = sem("dve_setup")
        s_plain_hi = sem("plain_hi")
        s_plain_lo = sem("plain_lo")
        s_edge_used = sem("edge_used")
        s_small_ready = sem("small_ready")
        s_group = sem("setup_group")
        s_group_hi = sem("setup_group_hi")
        s_group_out = sem("setup_group_out")
        s_setup_dve = sem("setup_dve_done")

        names = """
            x0_loaded res_loaded adj0_loaded blocks_loaded adj2_loaded out_stored
            x0T_mm x0T_hi x0T_lo hop1_mm edge_mm diag0 edge_i edge_bc_mm edge_sum edge_lrelu edge_exp
            alpha0 den0 inv0 trans0 trans0T_mm trans0T_hi trans0T_lo hop2_mm y2_hi y2_lo
            hop12_mm y1_hi y1_lo hop_mm
            adjT_mm adjT_hi adjT_lo split1_hi split1_lo feat_mm feat_hi feat_lo
            node_mm node_hi node_lo gcn_mm
            x2T_mm x2T_hi x2T_lo query_mm query_hi query_lo value_mm value_hi value_lo
            scores_mm rowbias2 exp2 attn2 inv2 probs2 probs2T_mm probs2T_hi probs2T_lo mix_mm
            x3T_mm x3T_hi x3T_lo value3_mm qk3_mm q3 k3_hi k3_lo nbr3_mm w3 diag3 w3_bc_mm
            max3 neg3 exp3_all exp3 inv3 gate3
        """.split()
        s = {n: sem(n) for n in names}
        s_sum = [sem(f"sum{l}") for l in range(LAYERS)]
        s_stats = [sem(f"stats{l}") for l in range(LAYERS)]
        s_moments = [sem(f"moments{l}") for l in range(LAYERS)]
        s_vareps = [sem(f"vareps{l}") for l in range(LAYERS)]
        s_rstd = [sem(f"rstd{l}") for l in range(LAYERS)]
        s_x = [sem(f"x{l + 1}") for l in range(LAYERS)]

        class Step:

            def __init__(self, t):
                self.t = t

            def on(self, layer):
                return not isinstance(self.t, int) or 0 <= self.t - layer < PAIRS

            def now(self, layer):
                n = self.t - layer + 1
                return max(0, min(n, PAIRS)) if isinstance(n, int) else n

            def before(self, layer):
                n = self.t - layer
                return max(0, min(n, PAIRS)) if isinstance(n, int) else n

        def run_steps(eng, body):
            for t in range(LAYERS):
                body(Step(t))
            with eng.Fori(LAYERS, PAIRS - 1) as t:
                body(Step(t))
            for t in range(PAIRS - 1, PAIRS + LAYERS - 1):
                body(Step(t))

        block = ctx.enter_context(nc.Block())

        @block.sync
        def _(sp):
            for row, b in ((0, bk0[0]), (2, bk0[1]), (4, bk0[2]), (6, b1), (8, b2), (10, b3), (12, bv2)):
                if row == 0:
                    sp.wait_ge(s_pool_const, 1)
                sp.dma_start(bias_raw[row:row + 2, :], b.rearrange("(a n) -> a n", a=1).broadcast_to([2, D])) \
                    .then_inc(s_vec_loaded, 16)
            sp.dma_start(aw_all[:], aw0.rearrange("(a n) b -> b a n", a=2).broadcast_to([P, 2, D])).then_inc(s_vec_loaded, 16)
            sp.dma_start(bv_all[:], bv0.rearrange("(a n) -> a n", a=1).broadcast_to([P, D])).then_inc(s_vec_loaded, 16)
            sp.dma_start(ab_all[:], ab0.rearrange("(a n) -> a n", a=1).broadcast_to([P, 1])).then_inc(s_vec_loaded, 16)
            sp.dma_start(bq_col[:], bq2.rearrange("(c p) -> p c", p=P), allow_slow_non_contiguous=True) \
                .then_inc(s_vec_loaded, 16)
            sp.dma_start(bk_col[:], bk2.rearrange("(c p) -> p c", p=P), allow_slow_non_contiguous=True) \
                .then_inc(s_vec_loaded, 16)
            matrices = [Wv0, Wk0[1], Wk0[2], Wk0[0], W1, W2, W3, Wq2, Wk2, Wv2, Wv3]
            for i, w in enumerate(matrices):
                if i == SLOTS:
                    sp.wait_ge(s_edge_used, 1)
                elif i > SLOTS:
                    sp.wait_ge(s_plain_lo, i - SLOTS)
                sp.dma_start(raw[i % SLOTS][:], w.rearrange("(c p) n -> p c n", p=P)).then_inc(s_slot[i % SLOTS], 16)
            i = len(matrices)
            sp.wait_ge(s_plain_lo, i - SLOTS)
            sp.dma_start(raw[i % SLOTS][:, 0, :], Wqk3).then_inc(s_slot[i % SLOTS], 16)

            sp.wait_ge(s_setup_dve, 1)
            sp.wait_ge(s_group, SETUP_GROUPS)
            sp.dma_start(x0_in[:], x_pairs[0]).then_inc(s["x0_loaded"], 16)
            sp.dma_start(adj0[:], adj_pairs[0]).then_inc(s["adj0_loaded"], 16)
            sp.wait_ge(s_pool_const, 4)

            def body(st):
                t = st.t
                if st.on(0):
                    wait(sp, s_sum[0], st.before(0))
                    sp.dma_start(x0_res[:], x_pairs[t]).then_inc(s["res_loaded"], 16)
                nxt = Step(t + 1)
                if nxt.on(0):
                    if st.on(0):
                        wait(sp, s["x0T_mm"], st.now(0))
                        sp.dma_start(x0_in[:], x_pairs[t + 1]).then_inc(s["x0_loaded"], 16)
                        wait(sp, s["alpha0"], st.now(0))
                        sp.dma_start(adj0[:], adj_pairs[t + 1]).then_inc(s["adj0_loaded"], 16)
                if not isinstance(t, int) or t <= PAIRS + LAYERS - 3:
                    wait(sp, s["adjT_mm"], t)
                    for slot, layer in ((0, 1), (1, 3)):
                        if nxt.on(layer):
                            for g in range(2):
                                sp.dma_start(adj_blocks[HALVES[g], slot, HALVES[g]],
                                             adj_graphs[t + 1 - layer, g]).then_inc(s["blocks_loaded"], 16)
                if nxt.on(2):
                    wait(sp, s["attn2"], st.now(2))
                    sp.dma_start(adj2[:], adj_pairs[t - 1]).then_inc(s["adj2_loaded"], 16)
                if st.on(3):
                    sp.wait_ge(s_x[3], st.now(3))
                    sp.dma_start(out_pairs[t - 3], x4[:]).then_inc(s["out_stored"], 16)

            run_steps(sp, body)
            sp.wait_ge(s["out_stored"], 16 * PAIRS)

        @block.gpsimd
        def _(pool):
            nc.gpsimd.memset(bias_raw[:], 0.0).then_inc(s_pool_const, 1)
            nc.gpsimd.memset(ident[:], 0.0).then_inc(s_pool_const, 1)
            pool.wait_ge(s_pool_const, 2)
            nc.gpsimd.affine_select(out=ident[:], in_=ident[:], compare_op=ALU.not_equal, fill=1.0,
                                    base=0, pattern=[[-1, P]], channel_multiplier=1).then_inc(s_pool_const, 1)
            nc.gpsimd.memset(minus_half, -0.5)
            pool.wait_ge(s_setup_dve, 1)
            pool.wait_ge(s_group, SETUP_GROUPS)
            nc.gpsimd.memset(trans0[:], 0.0)
            nc.gpsimd.memset(probs2[:], 0.0)
            nc.gpsimd.memset(adj_blocks[:], 0.0).then_inc(s_pool_const, 1)

            def inv_std(layer, count):
                pool.wait_ge(s_vareps[layer], count)
                nc.gpsimd.tensor_tensor(rstd[layer], var_eps[layer], minus_half, ALU.pow).then_inc(s_rstd[layer], 1)

            def body(st):
                if st.on(1):
                    wait(pool, s["feat_mm"], 3 * st.before(1))
                    pool.wait_ge(s["split1_hi"], st.now(1))
                    nc.gpsimd.tensor_tensor(node1[:, L], x1[:], node1[:, H].bitcast(F32), ALU.subtract) \
                        .then_inc(s["split1_lo"], 1)
                for layer in (3, 2, 1, 0):
                    if st.on(layer):
                        inv_std(layer, st.now(layer))

            run_steps(pool, body)

        def blocks_wait(eng, st):
            if isinstance(st.t, int):
                loads = 2 * (min(st.t + 1, PAIRS) + max(0, min(st.t - 1, PAIRS)))
            else:
                loads = 2 * (2 * st.t)
            eng.wait_ge(s["blocks_loaded"], 16 * loads)


        @block.tensor
        def _(pe):
            mm = nc.tensor.matmul

            group = [0]

            def begin():
                if group[0] >= 8:
                    pe.wait_ge(s_group_out, group[0] - 7)
                group[0] += 1
                return bank[(group[0] - 1) % 8]

            pe.wait_ge(s_slot[2], 32)
            pe.wait_ge(s_slot[3], 32)
            pe.wait_ge(s_small_ready, 1)
            rq, rk = raw[2], raw[3]
            for c in range(C):
                b = begin()
                for o in range(C):
                    last = mm(b[:], rq[:, o, c * P:(c + 1) * P], rk[:, o, :], start=o == 0, stop=o == C - 1)
                last.then_inc(s_group, 1)
            b = begin()
            for o in range(C):
                last = mm(b[0:16, :], bq_wide[:, o, :], rk[:, o, :], start=o == 0, stop=o == C - 1)
            last.then_inc(s_group, 1)
            b = begin()
            for c in range(C):
                for o in range(C):
                    last = mm(b[:, c:c + 1], rq[:, o, c * P:(c + 1) * P], bk_col[:, o:o + 1],
                              start=o == 0, stop=o == C - 1)
            last.then_inc(s_group, 1)
            b = begin()
            mm(b[:, 0:1], ones[:], sums[:, 0:1], start=True, stop=True).then_inc(s_group, 1)
            for slot, count in ((4, 32), (0, 48)):
                pe.wait_ge(s_slot[slot], count)
                for c in range(C):
                    b = begin()
                    for o in range(C):
                        last = nc.tensor.transpose(b[:, o * P:(o + 1) * P], raw[slot][:, o, c * P:(c + 1) * P], ident[:])
                    last.then_inc(s_group, 1)
            pe.wait_ge(s_slot[1], 48)
            b = begin()
            for c in range(C):
                last = nc.tensor.transpose(b[:, c * P:(c + 1) * P], raw[1][:, 0, c * P:(c + 1) * P], ident[:])
            last.then_inc(s_group, 1)
            assert group[0] == SETUP_GROUPS
            pe.wait_ge(s_group_out, SETUP_GROUPS)
            pe.wait_ge(s_setup_dve, 1)
            pe.wait_ge(s_plain_hi, len(plain))
            pe.wait_ge(s_plain_lo, len(plain))
            pe.wait_ge(s_pool_const, 4)

            def turn(dst, src):
                for c in range(C):
                    last = nc.tensor.transpose(dst[:, c * P:(c + 1) * P], src[:, c * P:(c + 1) * P], ident[:])
                return last

            def rows_times(dst, xT, w, start=True, stop=True):
                for c in range(C):
                    for i, (a, b) in enumerate(PASSES):
                        last = mm(dst, xT[:, a, c, :], w[:, b, c, :], start=start and c == 0 and i == 0,
                                  stop=stop and c == C - 1 and i == 2)
                return last

            def mix(dst, mT, y, start=True, stop=True):
                for i, (a, b) in enumerate(PASSES):
                    last = mm(dst, mT[:, a], y[:, b], start=start and i == 0, stop=stop and i == 2)
                return last

            def add_bias(dst, name):
                return mm(dst, select[name][:], bias_rows[:], start=False, stop=True)

            def neighbours(dst):
                for c in range(C):
                    for i, (a, b) in enumerate(PASSES):
                        last = mm(dst[:, c * P:(c + 1) * P], node1[:, a, c * P:(c + 1) * P], adjT[:, b, 0, :],
                                  start=i == 0, stop=i == 2)
                return last

            def gcn(w, name, sem_done):
                rows_times(bank[NODE1][:], feat1, w, stop=False)
                add_bias(bank[NODE1][:], name).then_inc(sem_done, 1)

            def turn_x0(count):
                pe.wait_ge(s["x0_loaded"], 16 * count)
                turn(bank[TURN], x0_in).then_inc(s["x0T_mm"], 1)

            def body(st):
                zero, one, two, three = (st.on(l) for l in range(LAYERS))
                n0, n1, n2, n3 = (st.now(l) for l in range(LAYERS))
                p0, p1, p2, p3 = (st.before(l) for l in range(LAYERS))

                if zero:
                    pe.wait_ge(s["x0T_hi"], n0)
                    pe.wait_ge(s["x0T_lo"], n0)
                    wait(pe, s["y1_lo"], p0)
                    rows_times(bank[HOP1][:], x0T, w_hop1, stop=False).then_inc(s["hop1_mm"], 1)
                if three:
                    pe.wait_ge(s_x[2], n3)
                    wait(pe, s["x0T_lo"], n0)
                    turn(bank[TURN], x3).then_inc(s["x3T_mm"], 1)
                if zero:
                    wait(pe, s["adjT_lo"], st.t)
                    for c in range(C):
                        for i, (a, b) in enumerate(PASSES):
                            last = mm(bank[SMALL][:, 0:2], x0T[:, a, c, :], w_edge[:, b, c, :],
                                      start=c == 0 and i == 0, stop=c == C - 1 and i == 2)
                    last.then_inc(s["edge_mm"], 1)
                    wait(pe, s_sum[0], p0)
                    rows_times(bank[HOP0][:], x0T, w_hop2).then_inc(s["hop2_mm"], 1)
                if two:
                    pe.wait_ge(s_x[1], n2)
                    wait(pe, s["x0T_lo"], n0)
                    wait(pe, s["x3T_lo"], n3)
                    turn(bank[TURN], x2).then_inc(s["x2T_mm"], 1)
                if zero:
                    pe.wait_ge(s["diag0"], n0)
                    pe.wait_ge(s["edge_i"], n0)
                    mm(bank[SMALL][:, 0:N], same_graph[:], diag0[:], start=True, stop=True).then_inc(s["edge_bc_mm"], 1)
                if one:
                    pe.wait_ge(s["split1_hi"], n1)
                    pe.wait_ge(s["split1_lo"], n1)
                    pe.wait_ge(s["adjT_hi"], st.t)
                    pe.wait_ge(s["adjT_lo"], st.t)
                    wait(pe, s["feat_lo"], 3 * p1)
                    neighbours(bank[FEAT1]).then_inc(s["feat_mm"], 1)
                if three:
                    pe.wait_ge(s["x3T_hi"], n3)
                    pe.wait_ge(s["x3T_lo"], n3)
                    wait(pe, s_sum[2], p2)
                    rows_times(bank[WIDE][:], x3T, w_v3).then_inc(s["value3_mm"], 1)
                    pe.wait_ge(s["adjT_lo"], st.t)
                    wait(pe, s["edge_sum"], n0)
                    rows_times(bank[SMALL][:, 0:2 * E3], x3T, w_qk3).then_inc(s["qk3_mm"], 1)
                if one:
                    pe.wait_ge(s["feat_hi"], 3 * p1 + 1)
                    pe.wait_ge(s["feat_lo"], 3 * p1 + 1)
                    wait(pe, s_sum[1], p1)
                    gcn(w_gcn1, "gcn1", s["node_mm"])
                if three:
                    pe.wait_ge(s["k3_hi"], n3)
                    pe.wait_ge(s["k3_lo"], n3)
                    for i, (a, b) in enumerate(PASSES):
                        last = mm(bank[SMALL][:, 0:E3], adjT[:, a, 1, :], k3[:, b], start=i == 0, stop=i == 2)
                    last.then_inc(s["nbr3_mm"], 1)
                if zero:
                    pe.wait_ge(s["trans0"], n0)
                    wait(pe, s["x2T_lo"], n2)
                    wait(pe, s["x3T_lo"], n3)
                    nc.tensor.transpose(bank[TURN][:, 0:P], trans0[:], ident[:]).then_inc(s["trans0T_mm"], 1)
                if two:
                    pe.wait_ge(s["x2T_hi"], n2)
                    pe.wait_ge(s["x2T_lo"], n2)
                    wait(pe, s["query_lo"], p2)
                    rows_times(bank[MID2][:], x2T, w_v2, stop=False)
                    add_bias(bank[MID2][:], "v2").then_inc(s["value_mm"], 1)
                if zero:
                    pe.wait_ge(s["trans0T_hi"], n0)
                    pe.wait_ge(s["trans0T_lo"], n0)
                    pe.wait_ge(s["y2_hi"], n0)
                    pe.wait_ge(s["y2_lo"], n0)
                    mix(bank[HOP1][:], trans0T, hop_y, start=False).then_inc(s["hop12_mm"], 1)
                if one:
                    pe.wait_ge(s["node_hi"], 2 * p1 + 1)
                    pe.wait_ge(s["node_lo"], 2 * p1 + 1)
                    neighbours(bank[FEAT1]).then_inc(s["feat_mm"], 1)
                if two:
                    pe.wait_ge(s["value_lo"], n2)
                    for f in range(C):
                        fs = slice(f * P, (f + 1) * P)
                        for c in range(C):
                            for i, (a, b) in enumerate(PASSES):
                                mm(bank[MID2][:, fs], w_qk2[:, a, c, fs], x2T[:, b, c, :],
                                   start=c == 0 and i == 0, stop=False)
                        last = mm(bank[MID2][:, fs], bias_rows[:, fs], select["key2"][:], start=False, stop=True)
                    last.then_inc(s["query_mm"], 1)
                if three:
                    pe.wait_ge(s["diag3"], n3)
                    mm(bank[SMALL][:, 0:N], same_graph[:], diag3[:], start=True, stop=True).then_inc(s["w3_bc_mm"], 1)
                if one:
                    pe.wait_ge(s["feat_hi"], 3 * p1 + 2)
                    pe.wait_ge(s["feat_lo"], 3 * p1 + 2)
                    gcn(w_gcn2, "gcn2", s["node_mm"])
                if two:
                    pe.wait_ge(s["query_hi"], n2)
                    pe.wait_ge(s["query_lo"], n2)
                    wait(pe, s["trans0T_lo"], n0)
                    for c in range(C):
                        for i, (a, b) in enumerate(PASSES):
                            mm(bank[TURN][:, 0:P], query2T[:, a, c, :], x2T[:, b, c, :],
                               start=c == 0 and i == 0, stop=c == C - 1 and i == 2)
                    for c in range(C):
                        for i, (a, b) in enumerate(PASSES):
                            last = mm(bank[TURN][:, P:P + 2], x2T[:, a, c, :], w_row2[:, b, c, :],
                                      start=c == 0 and i == 0, stop=c == C - 1 and i == 2)
                    last.then_inc(s["scores_mm"], 1)
                if zero:
                    pe.wait_ge(s["y2_lo"], n0)
                    rows_times(bank[HOP0][:], x0T, w_hop0, stop=False)
                if one:
                    pe.wait_ge(s["node_hi"], 2 * p1 + 2)
                    pe.wait_ge(s["node_lo"], 2 * p1 + 2)
                    neighbours(bank[FEAT1]).then_inc(s["feat_mm"], 1)
                if two:
                    pe.wait_ge(s["probs2"], n2)
                    nc.tensor.transpose(bank[TURN][:, 0:P], probs2[:], ident[:]).then_inc(s["probs2T_mm"], 1)
                if zero:
                    pe.wait_ge(s["y1_hi"], n0)
                    pe.wait_ge(s["y1_lo"], n0)
                    mix(bank[HOP0][:], trans0T, hop_y, start=False, stop=False)
                    add_bias(bank[HOP0][:], "hop").then_inc(s["hop_mm"], 1)
                if not isinstance(st.t, int) or st.t <= PAIRS + LAYERS - 3:
                    blocks_wait(pe, st)
                    wait(pe, s["exp3_all"], n3)
                    if not three:
                        wait(pe, s["edge_sum"], n0)
                        wait(pe, s["adjT_lo"], st.t)
                    for slot in range(2):
                        last = nc.tensor.transpose(bank[SMALL][:, slot * P:(slot + 1) * P], adj_blocks[:, slot, :], ident[:])
                    last.then_inc(s["adjT_mm"], 1)
                if Step(st.t + 1).on(0) and zero:
                    wait(pe, s["probs2T_lo"], n2)
                    if not two:
                        pe.wait_ge(s["trans0T_lo"], n0)
                    turn_x0(st.t + 2)
                if two:
                    pe.wait_ge(s["probs2T_hi"], n2)
                    pe.wait_ge(s["probs2T_lo"], n2)
                    wait(pe, s_sum[3], n3)
                    wait(pe, s_sum[2], p2)
                    mix(bank[WIDE][:], probs2T, value2).then_inc(s["mix_mm"], 1)
                if one:
                    pe.wait_ge(s["feat_hi"], 3 * p1 + 3)
                    pe.wait_ge(s["feat_lo"], 3 * p1 + 3)
                    gcn(w_gcn3, "gcn3", s["gcn_mm"])

            turn_x0(1)
            run_steps(pe, body)

        @block.scalar
        def _(act):
            def copy(dst, src):
                return nc.scalar.activation(dst, src, ACT.Copy)

            for i, w in enumerate(plain):
                slot, turn_ = (i + 1) % SLOTS, (i + 1) // SLOTS + 1
                act.wait_ge(s_slot[slot], 16 * turn_)
                copy(w[:, H], raw[slot][:]).then_inc(s_plain_hi, 1)
            group = 0
            for dst in ([w_qk2[:, H, c, :] for c in range(C)] + [None] * 3
                        + [w_v2[:, H, c, :] for c in range(C)] + [w_v3[:, H, c, :] for c in range(C)]
                        + [w_qk3[:, H, :, :]]):
                group += 1
                if dst is None:
                    continue
                act.wait_ge(s_group, group)
                src = bank[(group - 1) % 8][:]
                if group == SETUP_GROUPS:
                    src = src.rearrange("p (c n) -> p c n", c=C)
                copy(dst, src).then_inc(s_group_hi, 1)
            act.wait_ge(s_setup_dve, 1)

            def high(dst, src, ready, ready_count, done):
                act.wait_ge(ready, ready_count)
                copy(dst, src).then_inc(done, 1)

            def chunks(b):
                return bank[b][:].rearrange("p (c n) -> p c n", c=C)

            def turn_x0(count):
                act.wait_ge(s["x0T_mm"], count)
                wait(act, s["hop_mm"], count - 1)
                copy(x0T[:, H], chunks(TURN)).then_inc(s["x0T_hi"], 1)

            def body(st):
                zero, one, two, three = (st.on(l) for l in range(LAYERS))
                n0, n1, n2, n3 = (st.now(l) for l in range(LAYERS))
                p0, p1, p2, p3 = (st.before(l) for l in range(LAYERS))
                if three:
                    wait(act, s["qk3_mm"], p3)
                    high(x3T[:, H], chunks(TURN), s["x3T_mm"], n3, s["x3T_hi"])
                if zero:
                    wait(act, s["hop_mm"], p0)
                    high(hop_y[:, H], bank[HOP0][:], s["hop2_mm"], n0, s["y2_hi"])
                if one:
                    act.wait_ge(s_x[0], n1)
                    wait(act, s["feat_mm"], 3 * p1)
                    copy(node1[:, H], x1[:]).then_inc(s["split1_hi"], 1)
                if two:
                    wait(act, s["scores_mm"], p2)
                    high(x2T[:, H], chunks(TURN), s["x2T_mm"], n2, s["x2T_hi"])
                if one:
                    wait(act, s["gcn_mm"], p1)
                    high(feat1[:, H], chunks(FEAT1), s["feat_mm"], 3 * p1 + 1, s["feat_hi"])
                if zero:
                    act.wait_ge(s["edge_lrelu"], n0)
                    nc.scalar.activation(edge0[:], edge0[:], ACT.Exp).then_inc(s["edge_exp"], 1)
                if three:
                    wait(act, s["w3"], p3)
                    act.wait_ge(s["qk3_mm"], n3)
                    copy(q3[:], bank[SMALL][:, 0:E3]).then_inc(s["q3"], 1)
                    wait(act, s["nbr3_mm"], p3)
                    copy(k3[:, H], bank[SMALL][:, E3:2 * E3]).then_inc(s["k3_hi"], 1)
                if one:
                    act.wait_ge(s["node_mm"], 2 * p1 + 1)
                    act.wait_ge(s["feat_mm"], 3 * p1 + 1)
                    nc.scalar.activation(node1[:, H], bank[NODE1][:], ACT.Relu).then_inc(s["node_hi"], 1)
                if zero:
                    wait(act, s["hop_mm"], p0)
                    high(trans0T[:, H], bank[TURN][:, 0:P], s["trans0T_mm"], n0, s["trans0T_hi"])
                if two:
                    wait(act, s["mix_mm"], p2)
                    high(value2[:, H], bank[MID2][:], s["value_mm"], n2, s["value_hi"])
                if zero:
                    high(hop_y[:, H], bank[HOP1][:], s["hop12_mm"], n0, s["y1_hi"])
                if one:
                    act.wait_ge(s["node_mm"], 2 * p1 + 1)
                    high(feat1[:, H], chunks(FEAT1), s["feat_mm"], 3 * p1 + 2, s["feat_hi"])
                if two:
                    wait(act, s["scores_mm"], p2)
                    high(query2T[:, H], chunks(MID2), s["query_mm"], n2, s["query_hi"])
                if three:
                    act.wait_ge(s["neg3"], n3)
                    nc.scalar.activation(work3[:], bank[SMALL][:, 0:N], ACT.Exp, bias=max3,
                                         accum_out=sum3).then_inc(s["exp3_all"], 1)
                    nc.scalar.activation(exp3, w3, ACT.Exp, bias=max3).then_inc(s["exp3"], 1)
                if one:
                    act.wait_ge(s["node_mm"], 2 * p1 + 2)
                    act.wait_ge(s["feat_mm"], 3 * p1 + 2)
                    nc.scalar.activation(node1[:, H], bank[NODE1][:], ACT.Relu).then_inc(s["node_hi"], 1)
                if two:
                    act.wait_ge(s["rowbias2"], n2)
                    wait(act, s["probs2"], p2)
                    for g in HALVES:
                        last = nc.scalar.activation(attn2[g, :], bank[TURN][g, g], ACT.Exp, bias=rowbias2[g, :])
                    last.then_inc(s["exp2"], 1)
                if one:
                    act.wait_ge(s["node_mm"], 2 * p1 + 2)
                    high(feat1[:, H], chunks(FEAT1), s["feat_mm"], 3 * p1 + 3, s["feat_hi"])
                if two:
                    wait(act, s["mix_mm"], p2)
                    high(probs2T[:, H], bank[TURN][:, 0:P], s["probs2T_mm"], n2, s["probs2T_hi"])
                if not isinstance(st.t, int) or st.t <= PAIRS + LAYERS - 3:
                    wait(act, s["feat_mm"], 3 * n1)
                    wait(act, s["nbr3_mm"], n3)
                    act.wait_ge(s["adjT_mm"], st.t + 1)
                    copy(adjT[:, H], bank[SMALL][:, 0:2 * P].rearrange("p (a n) -> p a n", a=2)) \
                        .then_inc(s["adjT_hi"], 1)
                if Step(st.t + 1).on(0) and zero:
                    turn_x0(st.t + 2)

            turn_x0(1)
            run_steps(act, body)

        @block.vector
        def _(dve):
            setup_step = [0]

            def link(ins):
                setup_step[0] += 1
                ins.then_inc(s_dve_setup, 1)
                dve.wait_ge(s_dve_setup, setup_step[0])

            ve = nc.vector
            ve.memset(ones[:], 1.0)
            ve.memset(bq_wide[:], 0.0)
            ve.memset(same_graph[:], 0.0)
            link(ve.memset(row_raw[:], 0.0))
            for g in HALVES:
                ve.memset(same_graph[g, g], 1.0)
            dve.wait_ge(s_vec_loaded, 16 * 12)
            dve.wait_ge(s_pool_const, 3)
            for r in range(2):
                ve.tensor_copy(bq_wide[:, :, 14 + r:15 + r], bq_col[:].rearrange("p (c a) -> p c a", a=1))
            link(ve.tensor_tensor_reduce(out=junk[:, 0:C], in0=bq_col[:], in1=bk_col[:], scale=1.0, scalar=0.0,
                                         op0=ALU.mult, op1=ALU.add, accum_out=sums[:, 0:1]))
            ve.tensor_tensor(node_ident[:], ident[:, 0:N], ident[:, N:P], ALU.add).then_inc(s_small_ready, 1)
            ve.tensor_reduce(even, ident[:, 0::2], AX.X, ALU.add)
            ve.tensor_reduce(odd, ident[:, 1::2], AX.X, ALU.add)
            for i, (a, b) in enumerate(BIAS_ROWS.values()):
                last = ve.tensor_reduce(pick[:, i:i + 1], ident[:, a:b], AX.X, ALU.add)
            link(last)
            for i, n in enumerate(BIAS_ROWS):
                ve.tensor_scalar(select[n][:], ones[:], pick[:, i:i + 1], None, ALU.mult)
            for a in range(2):
                last = ve.tensor_tensor_reduce(out=junk[:], in0=bv_all[:], in1=aw_all[:, a, :], scale=1.0, scalar=0.0,
                                               op0=ALU.mult, op1=ALU.add, accum_out=sums[:, 1 + a:2 + a])
                link(last)
            dve.wait_ge(s_slot[0], 16)
            for c in range(C):
                for a in range(2):
                    link(ve.tensor_tensor_reduce(out=junk[:], in0=raw[0][:, c, :], in1=aw_all[:, a, :], scale=1.0,
                                                 scalar=0.0, op0=ALU.mult, op1=ALU.add,
                                                 accum_out=edge_raw[:, c, a:a + 1]))
            link(ve.tensor_copy(w_edge[:, H], edge_raw[:]))
            ve.tensor_tensor(w_edge[:, L], edge_raw[:], w_edge[:, H].bitcast(F32), ALU.subtract).then_inc(s_edge_used, 1)
            link(ve.tensor_tensor(edge_const, sums[:, 1:2], sums[:, 2:3], ALU.add))
            link(ve.tensor_tensor(edge_const, edge_const, ab_all[:], ALU.add))
            for i, w in enumerate(plain):
                dve.wait_ge(s_plain_hi, i + 1)
                slot = (i + 1) % SLOTS
                ve.tensor_tensor(w[:, L], raw[slot][:], w[:, H].bitcast(F32), ALU.subtract).then_inc(s_plain_lo, 1)
            highs = 0
            for group, w in enumerate([(w_qk2, c) for c in range(C)] + [None] * 3
                                      + [(w_v2, c) for c in range(C)] + [(w_v3, c) for c in range(C)]
                                      + [(w_qk3, None)]):
                src = bank[group % 8]
                if w:
                    highs += 1
                    dve.wait_ge(s_group_hi, highs)
                    m, c = w
                    if c is None:
                        ve.tensor_tensor(m[:, L], src[:].rearrange("p (c n) -> p c n", c=C), m[:, H].bitcast(F32),
                                         ALU.subtract).then_inc(s_group_out, 1)
                    else:
                        ve.tensor_tensor(m[:, L, c, :], src[:], m[:, H, c, :].bitcast(F32), ALU.subtract) \
                            .then_inc(s_group_out, 1)
                    continue
                dve.wait_ge(s_group, group + 1)
                if group == C:
                    ve.tensor_tensor(bias_raw[0:16, :], bias_raw[0:16, :], src[0:16, :], ALU.add) \
                        .then_inc(s_group_out, 1)
                    dve.wait_ge(s_group_out, group + 1)
                    link(ve.tensor_copy(bias_high[:], bias_raw[:]))
                    link(ve.tensor_tensor(bias_raw[:], bias_raw[:], bias_high[:].bitcast(F32), ALU.subtract))
                    link(ve.tensor_scalar(bias_raw[:], bias_raw[:], odd, None, ALU.mult))
                    link(ve.scalar_tensor_tensor(out=bias_rows[:], in0=bias_high[:].bitcast(F32), scalar=even,
                                                 in1=bias_raw[:], op0=ALU.mult, op1=ALU.add))
                elif group == C + 1:
                    ve.tensor_copy(row_raw[:, :, 0:1], src[:, 0:C].rearrange("p (c a) -> p c a", a=1)) \
                        .then_inc(s_group_out, 1)
                    dve.wait_ge(s_group_out, group + 1)
                    link(ve.tensor_copy(w_row2[:, H], row_raw[:]))
                    link(ve.tensor_tensor(w_row2[:, L], row_raw[:], w_row2[:, H].bitcast(F32), ALU.subtract))
                else:
                    ve.tensor_copy(row_const, src[:, 0:1]).then_inc(s_group_out, 1)
            dve.wait_ge(s_group_out, SETUP_GROUPS)
            link(ve.memset(sums[:], 0.0))
            ve.memset(junk[:, 0:2], 0.0).then_inc(s_setup_dve, 1)

            def chunks(b):
                return bank[b][:].rearrange("p (c n) -> p c n", c=C)

            def low(dst, src, high, hi_done, hi_count, done):
                dve.wait_ge(hi_done, hi_count)
                ve.tensor_tensor(dst, src, high.bitcast(F32), ALU.subtract).then_inc(done, 1)

            def relu_low(count):
                dve.wait_ge(s["node_hi"], count)
                ve.scalar_tensor_tensor(out=node1[:, L], in0=bank[NODE1][:], scalar=0.0,
                                        in1=node1[:, H].bitcast(F32), op0=ALU.max, op1=ALU.subtract) \
                    .then_inc(s["node_lo"], 1)

            def diagonal_blocks(dst, src, scale, done):
                for g in HALVES:
                    last = ve.tensor_scalar(dst[g, g], src[g, :], scale[g, :], None, ALU.mult)
                last.then_inc(done, 1)

            def statistics(l, count):
                dve.wait_ge(s_sum[l], count)
                ve.bn_stats(stats[l], xs[l + 1][:]).then_inc(s_stats[l], 1)

            def moments_of(l, count):
                ve.bn_aggr(moments[l], stats[l]).then_inc(s_moments[l], 1)
                dve.wait_ge(s_moments[l], count)
                ve.tensor_scalar(var_eps[l], moments[l][:, 1:2], LN_EPS, None, ALU.add).then_inc(s_vareps[l], 1)

            def normalise(l, count):
                dve.wait_ge(s_rstd[l], count)
                ve.tensor_scalar(xs[l + 1][:], xs[l + 1][:], moments[l][:, 0:1], rstd[l], ALU.subtract, ALU.mult) \
                    .then_inc(s_x[l], 1)

            def turn_x0(count):
                wait(dve, s["hop_mm"], count - 1)
                low(x0T[:, L], chunks(TURN), x0T[:, H], s["x0T_hi"], count, s["x0T_lo"])

            def body(st):
                zero, one, two, three = (st.on(l) for l in range(LAYERS))
                n0, n1, n2, n3 = (st.now(l) for l in range(LAYERS))
                p0, p1, p2, p3 = (st.before(l) for l in range(LAYERS))
                if three:
                    low(x3T[:, L], chunks(TURN), x3T[:, H], s["x3T_hi"], n3, s["x3T_lo"])
                if zero:
                    dve.wait_ge(s["edge_mm"], n0)
                    ve.tensor_scalar(diag0[:], node_ident[:], bank[SMALL][:, 0:1], None, ALU.mult).then_inc(s["diag0"], 1)
                    ve.tensor_tensor(edge_i, bank[SMALL][:, 1:2], edge_const, ALU.add).then_inc(s["edge_i"], 1)
                    low(hop_y[:, L], bank[HOP0][:], hop_y[:, H], s["y2_hi"], n0, s["y2_lo"])
                if two:
                    low(x2T[:, L], chunks(TURN), x2T[:, H], s["x2T_hi"], n2, s["x2T_lo"])
                if zero:
                    dve.wait_ge(s["edge_bc_mm"], n0)
                    dve.wait_ge(s["edge_i"], n0)
                    ve.tensor_scalar(edge0[:], bank[SMALL][:, 0:N], edge_i, None, ALU.add).then_inc(s["edge_sum"], 1)
                    dve.wait_ge(s["edge_sum"], n0)
                    ve.scalar_tensor_tensor(out=edge0[:], in0=edge0[:], scalar=SLOPE, in1=edge0[:], op0=ALU.mult,
                                            op1=ALU.max).then_inc(s["edge_lrelu"], 1)
                if one:
                    low(feat1[:, L], chunks(FEAT1), feat1[:, H], s["feat_hi"], 3 * p1 + 1, s["feat_lo"])
                if zero:
                    dve.wait_ge(s["edge_exp"], n0)
                    dve.wait_ge(s["adj0_loaded"], 16 * n0)
                    ve.tensor_tensor_reduce(out=edge0[:], in0=edge0[:], in1=adj0[:], scale=1.0, scalar=0.0,
                                            op0=ALU.mult, op1=ALU.add, accum_out=rowsum0).then_inc(s["alpha0"], 1)
                    dve.wait_ge(s["alpha0"], n0)
                    ve.tensor_scalar(rowsum0, rowsum0, ROWSUM_EPS, None, ALU.add).then_inc(s["den0"], 1)
                    dve.wait_ge(s["den0"], n0)
                    ve.reciprocal(inv0, rowsum0).then_inc(s["inv0"], 1)
                    dve.wait_ge(s["inv0"], n0)
                    diagonal_blocks(trans0, edge0, inv0, s["trans0"])
                if three:
                    low(k3[:, L], bank[SMALL][:, E3:2 * E3], k3[:, H], s["k3_hi"], n3, s["k3_lo"])
                if one:
                    relu_low(2 * p1 + 1)
                if three:
                    dve.wait_ge(s["nbr3_mm"], n3)
                    dve.wait_ge(s["q3"], n3)
                    wait(dve, s["exp3_all"], p3)
                    wait(dve, s["exp3"], p3)
                    ve.tensor_tensor_reduce(out=work3[:], in0=q3[:], in1=bank[SMALL][:, 0:E3], scale=SCALE3, scalar=0.0,
                                            op0=ALU.mult, op1=ALU.add, accum_out=w3).then_inc(s["w3"], 1)
                    dve.wait_ge(s["w3"], n3)
                    ve.tensor_scalar(diag3[:], node_ident[:], w3, None, ALU.mult).then_inc(s["diag3"], 1)
                if zero:
                    low(trans0T[:, L], bank[TURN][:, 0:P], trans0T[:, H], s["trans0T_hi"], n0, s["trans0T_lo"])
                if two:
                    low(value2[:, L], bank[MID2][:], value2[:, H], s["value_hi"], n2, s["value_lo"])
                if zero:
                    low(hop_y[:, L], bank[HOP1][:], hop_y[:, H], s["y1_hi"], n0, s["y1_lo"])
                if one:
                    low(feat1[:, L], chunks(FEAT1), feat1[:, H], s["feat_hi"], 3 * p1 + 2, s["feat_lo"])
                if two:
                    low(query2T[:, L], chunks(MID2), query2T[:, H], s["query_hi"], n2, s["query_lo"])
                if three:
                    dve.wait_ge(s["w3_bc_mm"], n3)
                    ve.reduce_max(max3, bank[SMALL][:, 0:N], AX.X).then_inc(s["max3"], 1)
                    dve.wait_ge(s["max3"], n3)
                    ve.tensor_scalar(max3, max3, -1.0, None, ALU.mult).then_inc(s["neg3"], 1)
                    dve.wait_ge(s["exp3_all"], n3)
                    ve.reciprocal(inv3, sum3).then_inc(s["inv3"], 1)
                    dve.wait_ge(s["inv3"], n3)
                    dve.wait_ge(s["exp3"], n3)
                    ve.tensor_tensor(gate3, exp3, inv3, ALU.mult).then_inc(s["gate3"], 1)
                    dve.wait_ge(s["gate3"], n3)
                    dve.wait_ge(s["value3_mm"], n3)
                    wait(dve, s["out_stored"], 16 * p3)
                    ve.scalar_tensor_tensor(out=x4[:], in0=bank[WIDE][:], scalar=gate3, in1=x3[:], op0=ALU.mult,
                                            op1=ALU.add).then_inc(s_sum[3], 1)
                    statistics(3, n3)
                    dve.wait_ge(s_stats[3], n3)
                if one:
                    relu_low(2 * p1 + 2)
                if three:
                    moments_of(3, n3)
                if two:
                    dve.wait_ge(s["scores_mm"], n2)
                    ve.tensor_tensor(rowbias2, bank[TURN][:, P:P + 1], row_const, ALU.add).then_inc(s["rowbias2"], 1)
                    dve.wait_ge(s["exp2"], n2)
                    dve.wait_ge(s["adj2_loaded"], 16 * n2)
                    ve.tensor_tensor_reduce(out=attn2[:], in0=attn2[:], in1=adj2[:], scale=1.0, scalar=0.0,
                                            op0=ALU.mult, op1=ALU.add, accum_out=rowsum2).then_inc(s["attn2"], 1)
                    dve.wait_ge(s["attn2"], n2)
                    ve.reciprocal(inv2, rowsum2).then_inc(s["inv2"], 1)
                    dve.wait_ge(s["inv2"], n2)
                    diagonal_blocks(probs2, attn2, inv2, s["probs2"])
                if three:
                    normalise(3, n3)
                if one:
                    low(feat1[:, L], chunks(FEAT1), feat1[:, H], s["feat_hi"], 3 * p1 + 3, s["feat_lo"])
                if two:
                    low(probs2T[:, L], bank[TURN][:, 0:P], probs2T[:, H], s["probs2T_hi"], n2, s["probs2T_lo"])
                if not isinstance(st.t, int) or st.t <= PAIRS + LAYERS - 3:
                    low(adjT[:, L], bank[SMALL][:, 0:2 * P].rearrange("p (a n) -> p a n", a=2), adjT[:, H],
                        s["adjT_hi"], st.t + 1, s["adjT_lo"])
                if Step(st.t + 1).on(0) and zero:
                    turn_x0(st.t + 2)
                if two:
                    dve.wait_ge(s["mix_mm"], n2)
                    ve.tensor_tensor(x3[:], bank[WIDE][:], x2[:], ALU.add).then_inc(s_sum[2], 1)
                    statistics(2, n2)
                    dve.wait_ge(s_stats[2], n2)
                if one:
                    dve.wait_ge(s["gcn_mm"], n1)
                    ve.tensor_tensor(x2[:], bank[NODE1][:], x1[:], ALU.add).then_inc(s_sum[1], 1)
                if two:
                    moments_of(2, n2)
                if one:
                    statistics(1, n1)
                    dve.wait_ge(s_stats[1], n1)
                if zero:
                    dve.wait_ge(s["hop_mm"], n0)
                    dve.wait_ge(s["res_loaded"], 16 * n0)
                    wait(dve, s["split1_lo"], n1)
                    wait(dve, s_sum[1], n1)
                    ve.scalar_tensor_tensor(out=x1[:], in0=bank[HOP0][:], scalar=0.0, in1=x0_res[:], op0=ALU.max,
                                            op1=ALU.add).then_inc(s_sum[0], 1)
                if one:
                    moments_of(1, n1)
                if zero:
                    statistics(0, n0)
                if two:
                    normalise(2, n2)
                if zero:
                    dve.wait_ge(s_stats[0], n0)
                if one:
                    normalise(1, n1)
                if zero:
                    moments_of(0, n0)
                    normalise(0, n0)

            turn_x0(1)
            run_steps(dve, body)


_INS = ['x', 'adj', 'L0_gnn_Wv', 'L0_gnn_bv', 'L0_gnn_aw', 'L0_gnn_ab', 'L0_gnn_Wk', 'L0_gnn_bk',
        'L1_gnn_W1', 'L1_gnn_b1', 'L1_gnn_W2', 'L1_gnn_b2', 'L1_gnn_W3', 'L1_gnn_b3',
        'L2_gnn_Wq_w', 'L2_gnn_Wq_b', 'L2_gnn_Wk_w', 'L2_gnn_Wk_b', 'L2_gnn_Wv_w', 'L2_gnn_Wv_b',
        'L3_gnn_W_qk', 'L3_gnn_W_v']


def kernel(**inputs):
    import numpy as _np
    import concourse.bacc as _bacc
    from concourse import mybir as _mybir
    from concourse.bass_utils import run_bass_kernel_spmd as _run

    nc = _bacc.Bacc("TRN2", target_bir_lowering=False, num_devices=1)
    arrays, args = {}, []
    for name in _INS:
        a = _np.ascontiguousarray(inputs[name])
        arrays[f"in_{name}_dram"] = a
        args.append(nc.dram_tensor(f"in_{name}_dram", a.shape, _mybir.dt.from_np(a.dtype), kind="ExternalInput").ap())
    args.append(nc.dram_tensor("out_0_dram", inputs["x"].shape, _mybir.dt.float32, kind="ExternalOutput").ap())
    build(nc, *args)
    r = _run(nc, [arrays], core_ids=[0])
    return r.results[0]["out_0_dram"]
```

```python
from contextlib import ExitStack

import concourse.bass as bass
from concourse import mybir

F32 = mybir.dt.float32
F32R = mybir.dt.float32r
ALU = mybir.AluOpType
ACT = mybir.ActivationFunctionType
AX = mybir.AxisListType

H, L = 0, 1
PASSES = ((H, H), (H, L), (L, H))
P = 128
LAYERS = 4
LN_EPS = 1e-5
ROWSUM_EPS = 1e-12
SLOPE = 0.2


def wait(eng, sem, count):
    if isinstance(count, int) and count <= 0:
        return
    eng.wait_ge(sem, count)


def build(nc, x, adj, Wv0, bv0, aw0, ab0, Wk0, bk0, W1, b1, W2, b2, W3, b3,
          Wq2, bq2, Wk2, bk2, Wv2, bv2, Wqk3, Wv3, out):
    graphs, N, D = x.shape
    C = D // P
    PAIRS = graphs * N // P
    E3 = Wqk3.shape[0] // 2
    SCALE3 = float(E3) ** -0.5
    HALVES = (slice(0, N), slice(N, P))
    assert 2 * N == P and D == 512 and 2 * E3 == P and PAIRS > 2 * LAYERS - 2

    x_pairs = x.rearrange("(t g) n d -> t (g n) d", g=2)
    out_pairs = out.rearrange("(t g) n d -> t (g n) d", g=2)
    adj_pairs = adj.rearrange("(t g) i j -> t (g i) j", g=2)
    adj_graphs = adj.rearrange("(t g) i j -> t g i j", g=2)

    with ExitStack() as ctx:
        def sb(name, shape, dt=F32):
            return ctx.enter_context(nc.sbuf_tensor(name, shape, dt))

        def sem(name):
            return ctx.enter_context(nc.semaphore(name))

        EDGE = ROW = 2
        w_hop1 = sb("w_hop1", [P, 2, C, D], F32R)
        w_hop2 = sb("w_hop2", [P, 2, C, D + EDGE], F32R)
        w_hop0 = sb("w_hop0", [P, 2, C, D], F32R)
        w_gcn1 = sb("w_gcn1", [P, 2, C, D], F32R)
        w_gcn2 = sb("w_gcn2", [P, 2, C, D], F32R)
        w_gcn3 = sb("w_gcn3", [P, 2, C, D], F32R)
        plain = [w_hop1, w_hop2, w_hop0, w_gcn1, w_gcn2, w_gcn3]
        w_qk2 = sb("w_qk2", [P, 2, C, D + ROW], F32R)
        w_v2 = sb("w_v2", [P, 2, C, D], F32R)
        w_v3 = sb("w_v3", [P, 2, C, D + 2 * E3], F32R)
        ident = sb("ident", [P, P])
        same_graph = sb("same_graph", [P, P])
        node_ident = sb("node_ident", [P, N])
        bias_rows = sb("bias_rows", [P, D], F32R)
        KEY_ROW = 10
        BIAS_ROWS = {"hop": (0, 6), "gcn1": (6, 8), "gcn2": (8, 10), "key2": (KEY_ROW, KEY_ROW + 2)}
        select = {n: sb(f"select_{n}", [P, P], F32R) for n in BIAS_ROWS}
        bias_gcn3 = sb("bias_gcn3", [P, D])
        bias_v2 = sb("bias_v2", [P, D])
        cols = sb("cols", [P, 96])
        used_cols = [0]

        def col(n=1):
            used_cols[0] += n
            return cols[:, used_cols[0] - n:used_cols[0]]

        edge_const = col()
        row_const = col()
        even, odd = col(), col()
        minus_half = col()
        pad = col()

        SLOTS = 5
        with ExitStack() as staging:
            def stage(name, shape, dt=F32):
                return staging.enter_context(nc.sbuf_tensor(name, shape, dt))

            raw = [stage(f"raw{i}", [P, C, D]) for i in range(SLOTS)]
            aw_all = stage("aw_all", [P, 2, D])
            bv_all = stage("bv_all", [P, D])
            bias_raw = stage("bias_raw", [P, D])
            ones = stage("ones", [P, P])
            bq_col = stage("bq_col", [P, C])
            bk_col = stage("bk_col", [P, C])
            bq_wide = stage("bq_wide", [P, C, 16])
            edge_raw = stage("edge_raw", [P, C, 2])
            row_raw = stage("row_raw", [P, C, 2])
            ab_all = stage("ab_all", [P, 1])
            pick = stage("pick", [P, len(BIAS_ROWS)])
            sums = stage("sums", [P, 3])

        x0_in = sb("x0_in", [P, D])
        x0T = sb("x0T", [P, 2, C, P], F32R)
        hop_y = sb("hop_y", [P, 2, D], F32R)
        adj0 = sb("adj0", [P, N])
        edge0 = work3 = sb("edge0", [P, N])
        diag0 = diag3 = sb("diag", [P, N])
        trans0 = sb("trans0", [P, P])
        trans0T = sb("trans0T", [P, 2, P], F32R)
        x1 = sb("x1", [P, D])
        x0_res = sb("x0_res", [P, D])
        relu1 = query2 = x0_res
        node1 = sb("node1", [P, 2, D], F32R)
        feat1 = sb("feat1", [P, 2, C, P], F32R)
        adj_blocks = sb("adj_blocks", [P, 2, P])
        adjT = sb("adjT", [P, 2, 2, P], F32R)
        x2 = sb("x2", [P, D])
        x2T = sb("x2T", [P, 2, C, P], F32R)
        query2T = sb("query2T", [P, 2, C, P], F32R)
        value2 = sb("value2", [P, 2, D], F32R)
        adj2 = sb("adj2", [P, N])
        attn2 = sb("attn2", [P, N])
        probs2 = sb("probs2", [P, P])
        probs2T = sb("probs2T", [P, 2, P], F32R)
        x3 = sb("x3", [P, D])
        x3T = sb("x3T", [P, 2, C, P], F32R)
        q3 = sb("q3", [P, E3])
        k3 = sb("k3", [P, 2, E3], F32R)
        sum_of = [x0_res, x2, x3, x3]
        edge_i = col()
        rowsum0, inv0 = col(), col()
        rowbias2 = col()
        rowsum2, inv2 = col(), col()
        w3, max3, exp3, sum3, inv3, gate3 = col(), col(), col(), col(), col(), col()
        stats = [col(6) for _ in range(LAYERS)]
        moments = [col(2) for _ in range(LAYERS)]
        var_eps = [col() for _ in range(LAYERS)]
        rstd = [col() for _ in range(LAYERS)]

        SETUP_GROUPS = C + 3 + 2 * C + 1

        BANK = 512
        bank = [ctx.enter_context(nc.psum_tensor(f"bank{i}", [P, BANK], F32)) for i in range(4)]
        pair_a = ctx.enter_context(nc.psum_tensor("pair_a", [P, 2 * BANK], F32))
        pair_b = ctx.enter_context(nc.psum_tensor("pair_b", [P, 2 * BANK], F32))
        hop1_ps, mid_ps, turn_ps, gcn_ps = (b[:] for b in bank)
        banks = [b[:] for b in bank] + [pair_a[:, 0:BANK], pair_a[:, BANK:], pair_b[:, 0:BANK], pair_b[:, BANK:]]
        LEAD_A, LEAD_B = D // 2, (D + 2 * E3) // 2
        junk = pair_b[:, BANK:]
        wide_a = pair_a[:, BANK - LEAD_A:BANK - LEAD_A + D + EDGE]
        wide_b = pair_b[:, BANK - LEAD_B:BANK - LEAD_B + D + 2 * E3]
        edge_bc_ps = pair_a[:, BANK:BANK + N]
        adjT_ps = pair_a[:, 0:2 * P]
        queryT_ps = pair_a[:, 0:BANK]
        scores_ps = pair_a[:, BANK:BANK + P]
        mix_ps = pair_b[:, 0:BANK]
        nbr3_ps = pair_b[:, 2 * BANK - 2 * N:2 * BANK - N]
        w3_bc_ps = pair_b[:, 2 * BANK - N:2 * BANK]

        s_slot = [sem(f"slot{i}") for i in range(SLOTS)]
        s_vec_loaded = sem("vec_loaded")
        s_pool_const = sem("pool_const")
        s_pool_lo = sem("pool_lo")
        s_dve_setup = sem("dve_setup")
        PLAIN_SLOT = ((3, 16), (4, 16), (2, 32), (3, 32), (4, 32), (2, 48))
        ON_POOL = 2
        s_plain_hi = sem("plain_hi")
        s_plain_lo = sem("plain_lo")
        s_edge_used = sem("edge_used")
        s_small_ready = sem("small_ready")
        s_group = sem("setup_group")
        s_group_hi = sem("setup_group_hi")
        s_group_out = sem("setup_group_out")
        s_setup_dve = sem("setup_dve_done")

        names = """
            x0_loaded res_loaded adj0_loaded blocks_loaded adj2_loaded out_stored
            x0T_mm x0T_hi x0T_lo hop2_mm diag0 edge_i edge_bc_mm edge_sum edge_lrelu edge_exp
            alpha0 den0 inv0 trans0 trans0T_mm trans0T_hi trans0T_lo y2_hi y2_lo
            hop12_mm y1_hi y1_lo hop0_mm hop_mm
            adjT_mm adjT_hi adjT_lo x1_bias x2_bias turn1_mm feat_hi feat_lo support_mm node_hi node_lo gcn_mm relu1
            x2T_mm x2T_hi x2T_lo query_mm query2 queryT_mm queryT_hi queryT_lo value_mm value_hi value_lo
            scores_mm rowbias2 exp2 attn2 inv2 probs2 probs2T_mm probs2T_hi probs2T_lo mix_mm
            x3T_mm x3T_hi x3T_lo value3_mm q3 k3_hi k3_lo nbr3_mm w3 diag3 w3_bc_mm
            max3 neg3 exp3_all exp3 inv3 gate3
        """.split()
        s = {n: sem(n) for n in names}
        s_sum = [sem(f"sum{l}") for l in range(LAYERS)]
        s_stats = [sem(f"stats{l}") for l in range(LAYERS)]
        s_moments = [sem(f"moments{l}") for l in range(LAYERS)]
        s_vareps = [sem(f"vareps{l}") for l in range(LAYERS)]
        s_rstd = [sem(f"rstd{l}") for l in range(LAYERS)]
        s_x = [sem(f"x{l + 1}") for l in range(LAYERS)]

        class Step:

            def __init__(self, t):
                self.t = t

            def on(self, layer):
                return not isinstance(self.t, int) or 0 <= self.t - layer < PAIRS

            def now(self, layer):
                n = self.t - layer + 1
                return max(0, min(n, PAIRS)) if isinstance(n, int) else n

            def before(self, layer):
                n = self.t - layer
                return max(0, min(n, PAIRS)) if isinstance(n, int) else n

            def pair_follows(self):
                return not isinstance(self.t, int) or self.t < PAIRS - 1

            def blocks_follow(self):
                return not isinstance(self.t, int) or self.t < PAIRS + LAYERS - 2

        def run_steps(eng, body):
            for t in range(LAYERS):
                body(Step(t))
            with eng.Fori(LAYERS, PAIRS - 1) as t:
                body(Step(t))
            for t in range(PAIRS - 1, PAIRS + LAYERS - 1):
                body(Step(t))

        block = ctx.enter_context(nc.Block())

        @block.sync
        def _(sp):
            sp.dma_start(bq_col[:], bq2.rearrange("(c p) -> p c", p=P), allow_slow_non_contiguous=True) \
                .then_inc(s_vec_loaded, 16)
            sp.dma_start(bk_col[:], bk2.rearrange("(c p) -> p c", p=P), allow_slow_non_contiguous=True) \
                .then_inc(s_vec_loaded, 16)

            def load(i):
                w, slot, free, count = matrices[i]
                if free is not None:
                    sp.wait_ge(free, count)
                dst = raw[slot][:, 0, :] if w.shape[0] == P else raw[slot][:]
                src = w if w.shape[0] == P else w.rearrange("(c p) n -> p c n", p=P)
                sp.dma_start(dst, src).then_inc(s_slot[slot], 16)

            matrices = [(Wq2, 0, None, 0), (Wk2, 1, None, 0), (Wv0, 2, None, 0), (Wk0[1], 3, None, 0),
                        (Wk0[2], 4, None, 0), (Wk0[0], 2, s_edge_used, 1), (W1, 3, s_plain_lo, 1),
                        (W2, 4, s_plain_lo, 2), (W3, 2, s_plain_lo, 3), (Wv2, 0, s_group, C + 2),
                        (Wv3, 1, s_group, C + 2), (Wqk3, 3, s_plain_lo, 4)]
            load(0)
            load(1)

            def row(v):
                return v.rearrange("(a n) -> a n", a=1)

            sp.dma_start(aw_all[:], aw0.rearrange("(a n) b -> b a n", a=2).broadcast_to([P, 2, D])).then_inc(s_vec_loaded, 16)
            sp.dma_start(bv_all[:], row(bv0).broadcast_to([P, D])).then_inc(s_vec_loaded, 16)
            sp.dma_start(ab_all[:], row(ab0).broadcast_to([P, 1])).then_inc(s_vec_loaded, 16)
            sp.dma_start(bias_gcn3[:], row(b3).broadcast_to([P, D])).then_inc(s_vec_loaded, 16)
            sp.dma_start(bias_v2[:], row(bv2).broadcast_to([P, D])).then_inc(s_vec_loaded, 16)
            sp.wait_ge(s_pool_const, 1)
            for at, b in ((0, bk0[0]), (2, bk0[1]), (4, bk0[2]), (6, b1), (8, b2)):
                sp.dma_start(bias_raw[at:at + 2, :], row(b).broadcast_to([2, D])).then_inc(s_vec_loaded, 16)
            for i in range(2, len(matrices)):
                load(i)

            sp.wait_ge(s_setup_dve, 1)
            sp.wait_ge(s_pool_lo, ON_POOL)
            sp.wait_ge(s_group, SETUP_GROUPS)
            sp.dma_start(x0_in[:], x_pairs[0]).then_inc(s["x0_loaded"], 16)
            sp.dma_start(adj0[:], adj_pairs[0]).then_inc(s["adj0_loaded"], 16)
            sp.wait_ge(s_pool_const, 4)

            def body(st):
                t = st.t
                nxt = Step(t + 1)
                if st.blocks_follow():
                    wait(sp, s["adjT_mm"], t)
                    for slot, layer in ((0, 1), (1, 3)):
                        if nxt.on(layer):
                            for g in range(2):
                                sp.dma_start(adj_blocks[HALVES[g], slot, HALVES[g]],
                                             adj_graphs[t + 1 - layer, g]).then_inc(s["blocks_loaded"], 16)
                if st.pair_follows():
                    wait(sp, s["x0T_mm"], st.now(0))
                    sp.dma_start(x0_in[:], x_pairs[t + 1]).then_inc(s["x0_loaded"], 16)
                    wait(sp, s["alpha0"], st.now(0))
                    sp.dma_start(adj0[:], adj_pairs[t + 1]).then_inc(s["adj0_loaded"], 16)
                if nxt.on(2):
                    wait(sp, s["attn2"], st.now(2))
                    sp.dma_start(adj2[:], adj_pairs[t - 1]).then_inc(s["adj2_loaded"], 16)
                if st.on(0):
                    wait(sp, s["turn1_mm"], 3 * st.now(1))
                    wait(sp, s["x1_bias"], st.now(1))
                    wait(sp, s["queryT_mm"], st.now(2))
                    sp.dma_start(x0_res[:], x_pairs[t]).then_inc(s["res_loaded"], 16)
                if st.on(3):
                    sp.wait_ge(s_x[3], st.now(3))
                    sp.dma_start(out_pairs[t - 3], x3[:]).then_inc(s["out_stored"], 16)

            run_steps(sp, body)
            sp.wait_ge(s["out_stored"], 16 * PAIRS)

        @block.gpsimd
        def _(pool):
            nc.gpsimd.memset(bias_raw[:], 0.0).then_inc(s_pool_const, 1)
            nc.gpsimd.memset(ident[:], 0.0).then_inc(s_pool_const, 1)
            pool.wait_ge(s_pool_const, 2)
            nc.gpsimd.affine_select(out=ident[:], in_=ident[:], compare_op=ALU.not_equal, fill=1.0,
                                    base=0, pattern=[[-1, P]], channel_multiplier=1).then_inc(s_pool_const, 1)
            nc.gpsimd.memset(minus_half, -0.5)
            for i in range(len(plain) - ON_POOL, len(plain)):
                w = plain[i]
                pool.wait_ge(s_plain_hi, i + 1)
                nc.gpsimd.tensor_tensor(w[:, L, :, 0:D], raw[PLAIN_SLOT[i][0]][:], w[:, H, :, 0:D].bitcast(F32),
                                        ALU.subtract).then_inc(s_pool_lo, 1)
            pool.wait_ge(s_setup_dve, 1)
            pool.wait_ge(s_group, SETUP_GROUPS)
            pool.wait_ge(s_vec_loaded, 16 * 12)
            nc.gpsimd.memset(trans0[:], 0.0)
            nc.gpsimd.memset(probs2[:], 0.0)
            nc.gpsimd.memset(adj_blocks[:], 0.0).then_inc(s_pool_const, 1)

            def inv_std(layer, count):
                pool.wait_ge(s_vareps[layer], count)
                nc.gpsimd.tensor_tensor(rstd[layer], var_eps[layer], minus_half, ALU.pow).then_inc(s_rstd[layer], 1)

            def body(st):
                n0, n1, n2, n3 = (st.now(l) for l in range(LAYERS))
                if st.on(1):
                    pool.wait_ge(s_x[0], n1)
                    wait(pool, s_sum[1], st.before(1))
                    nc.gpsimd.tensor_tensor(x1[:], x0_res[:], bias_gcn3[:], ALU.add).then_inc(s["x1_bias"], 1)
                if st.on(2):
                    pool.wait_ge(s["x2T_mm"], n2)
                    nc.gpsimd.tensor_tensor(x2[:], x2[:], bias_v2[:], ALU.add).then_inc(s["x2_bias"], 1)
                for layer, count in ((3, n3), (2, n2), (0, n0), (1, n1)):
                    if st.on(layer):
                        inv_std(layer, count)

            run_steps(pool, body)

        def blocks_wait(eng, st):
            if isinstance(st.t, int):
                loads = 2 * (min(st.t + 1, PAIRS) + max(0, min(st.t - 1, PAIRS)))
            else:
                loads = 2 * (2 * st.t)
            eng.wait_ge(s["blocks_loaded"], 16 * loads)


        @block.tensor
        def _(pe):
            mm = nc.tensor.matmul

            group = [0]

            def begin():
                if group[0] >= 8:
                    pe.wait_ge(s_group_out, group[0] - 7)
                if group[0] == 7:
                    pe.wait_ge(s_edge_used, 1)
                group[0] += 1
                return banks[(group[0] - 1) % 8]

            pe.wait_ge(s_slot[0], 16)
            pe.wait_ge(s_slot[1], 16)
            pe.wait_ge(s_small_ready, 1)
            rq, rk = raw[0], raw[1]
            for c in range(C):
                b = begin()
                for o in range(C):
                    last = mm(b, rq[:, o, c * P:(c + 1) * P], rk[:, o, :], start=o == 0, stop=o == C - 1)
                last.then_inc(s_group, 1)
            b = begin()
            for o in range(C):
                last = mm(b[0:16, :], bq_wide[:, o, :], rk[:, o, :], start=o == 0, stop=o == C - 1)
            last.then_inc(s_group, 1)
            b = begin()
            for c in range(C):
                for o in range(C):
                    last = mm(b[:, c:c + 1], rq[:, o, c * P:(c + 1) * P], bk_col[:, o:o + 1],
                              start=o == 0, stop=o == C - 1)
            last.then_inc(s_group, 1)
            b = begin()
            mm(b[:, 0:1], ones[:], sums[:, 0:1], start=True, stop=True).then_inc(s_group, 1)
            for slot, count in ((0, 32), (1, 32)):
                pe.wait_ge(s_slot[slot], count)
                for c in range(C):
                    b = begin()
                    for o in range(C):
                        last = nc.tensor.transpose(b[:, o * P:(o + 1) * P], raw[slot][:, o, c * P:(c + 1) * P], ident[:])
                    last.then_inc(s_group, 1)
            pe.wait_ge(s_slot[3], 48)
            b = begin()
            for c in range(C):
                last = nc.tensor.transpose(b[:, c * P:(c + 1) * P], raw[3][:, 0, c * P:(c + 1) * P], ident[:])
            last.then_inc(s_group, 1)
            assert group[0] == SETUP_GROUPS
            pe.wait_ge(s_group_out, SETUP_GROUPS)
            pe.wait_ge(s_setup_dve, 1)
            pe.wait_ge(s_plain_hi, len(plain))
            pe.wait_ge(s_plain_lo, len(plain) - ON_POOL)
            pe.wait_ge(s_pool_lo, ON_POOL)
            pe.wait_ge(s_pool_const, 4)

            def turn(dst, src):
                for c in range(C):
                    last = nc.tensor.transpose(dst[:, c * P:(c + 1) * P], src[:, c * P:(c + 1) * P], ident[:])
                return last

            def rows_times(dst, xT, w, chunks=range(C), stop=True):
                for c in chunks:
                    for i, (a, b) in enumerate(PASSES):
                        last = mm(dst, xT[:, a, c, :], w[:, b, c, :], start=c == 0 and i == 0,
                                  stop=stop and c == C - 1 and i == 2)
                return last

            def rows_times_wide(dst, xT, w, lead, stop=True):
                for c in range(C):
                    for i, (a, b) in enumerate(PASSES):
                        for part in (slice(0, lead), slice(lead, dst.shape[1])):
                            last = mm(dst[:, part], xT[:, a, c, :], w[:, b, c, part], start=c == 0 and i == 0,
                                      stop=stop and c == C - 1 and i == 2)
                return last

            def mix(dst, mT, y, start=True, stop=True):
                for i, (a, b) in enumerate(PASSES):
                    last = mm(dst, mT[a], y[:, b], start=start and i == 0, stop=stop and i == 2)
                return last

            def add_bias(dst, name, part=slice(0, D)):
                return mm(dst, select[name][:], bias_rows[:, part], start=False, stop=True)

            def high_low(t):
                return [t[:, H], t[:, L]]

            def support(count, w):
                pe.wait_ge(s["feat_hi"], count)
                pe.wait_ge(s["feat_lo"], count)
                rows_times(gcn_ps, feat1, w).then_inc(s["support_mm"], 1)

            def aggregate(count, bias):
                pe.wait_ge(s["node_hi"], count)
                pe.wait_ge(s["node_lo"], count)
                last = mix(gcn_ps, [adjT[:, a, 0, :] for a in (H, L)], node1, stop=bias is None)
                if bias is not None:
                    last = add_bias(gcn_ps, bias)
                last.then_inc(s["gcn_mm"], 1)

            def turn_relu(count):
                pe.wait_ge(s["relu1"], count)
                turn(gcn_ps, relu1).then_inc(s["turn1_mm"], 1)

            def turn_x0(count):
                pe.wait_ge(s["x0_loaded"], 16 * count)
                turn(turn_ps, x0_in).then_inc(s["x0T_mm"], 1)

            def begin_hop1(count):
                pe.wait_ge(s["x0T_hi"], count)
                pe.wait_ge(s["x0T_lo"], count)
                rows_times(hop1_ps, x0T, w_hop1, chunks=range(C - 1), stop=False)

            def body(st):
                zero, one, two, three = (st.on(l) for l in range(LAYERS))
                n0, n1, n2, n3 = (st.now(l) for l in range(LAYERS))
                p0, p1, p2, p3 = (st.before(l) for l in range(LAYERS))

                if zero:
                    rows_times(hop1_ps, x0T, w_hop1, chunks=range(C - 1, C), stop=False)
                if three:
                    pe.wait_ge(s_x[2], n3)
                    wait(pe, s["x0T_lo"], n0)
                    turn(turn_ps, x3).then_inc(s["x3T_mm"], 1)
                if one:
                    pe.wait_ge(s_x[0], n1)
                    wait(pe, s_sum[1], p1)
                    turn(gcn_ps, x0_res).then_inc(s["turn1_mm"], 1)
                if zero:
                    wait(pe, s["adjT_lo"], st.t)
                    wait(pe, s["exp2"], p2)
                    rows_times_wide(wide_a, x0T, w_hop2, LEAD_A).then_inc(s["hop2_mm"], 1)
                if two:
                    pe.wait_ge(s_x[1], n2)
                    wait(pe, s_sum[0], p0)
                    turn(mid_ps, x2).then_inc(s["x2T_mm"], 1)
                if one:
                    support(3 * p1 + 1, w_gcn1)
                if zero:
                    pe.wait_ge(s["diag0"], n0)
                    pe.wait_ge(s["edge_i"], n0)
                    pe.wait_ge(s["y2_lo"], n0)
                    mm(edge_bc_ps, same_graph[:], diag0[:], start=True, stop=True).then_inc(s["edge_bc_mm"], 1)
                if three:
                    pe.wait_ge(s["x3T_hi"], n3)
                    pe.wait_ge(s["x3T_lo"], n3)
                    wait(pe, s_sum[2], p2)
                    rows_times_wide(wide_b, x3T, w_v3, LEAD_B).then_inc(s["value3_mm"], 1)
                if one:
                    aggregate(3 * p1 + 1, "gcn1")
                if two:
                    pe.wait_ge(s["x2T_hi"], n2)
                    pe.wait_ge(s["x2T_lo"], n2)
                    wait(pe, s["y2_lo"], n0)
                    wait(pe, s["edge_sum"], n0)
                    rows_times_wide(wide_a, x2T, w_qk2, LEAD_A, stop=False)
                    add_bias(wide_a[:, 0:LEAD_A], "key2", slice(0, LEAD_A))
                    add_bias(wide_a[:, LEAD_A:D], "key2", slice(LEAD_A, D)).then_inc(s["query_mm"], 1)
                if one:
                    turn_relu(2 * p1 + 1)
                if three:
                    pe.wait_ge(s["q3"], n3)
                    pe.wait_ge(s["k3_hi"], n3)
                    pe.wait_ge(s["k3_lo"], n3)
                    for i, (a, b) in enumerate(PASSES):
                        last = mm(nbr3_ps, adjT[:, a, 1, :], k3[:, b], start=i == 0, stop=i == 2)
                    last.then_inc(s["nbr3_mm"], 1)
                if zero:
                    pe.wait_ge(s["trans0"], n0)
                    wait(pe, s["x3T_lo"], n3)
                    nc.tensor.transpose(turn_ps[:, 0:P], trans0[:], ident[:]).then_inc(s["trans0T_mm"], 1)
                if two:
                    rows_times(mid_ps, x2T, w_v2).then_inc(s["value_mm"], 1)
                if three:
                    pe.wait_ge(s["diag3"], n3)
                    mm(w3_bc_ps, same_graph[:], diag3[:], start=True, stop=True).then_inc(s["w3_bc_mm"], 1)
                if one:
                    support(3 * p1 + 2, w_gcn2)
                if two:
                    pe.wait_ge(s["query2"], n2)
                    pe.wait_ge(s["rowbias2"], n2)
                    turn(queryT_ps, query2).then_inc(s["queryT_mm"], 1)
                if zero:
                    pe.wait_ge(s["trans0T_hi"], n0)
                    pe.wait_ge(s["trans0T_lo"], n0)
                    pe.wait_ge(s["y2_hi"], n0)
                    mix(hop1_ps, high_low(trans0T), hop_y, start=False).then_inc(s["hop12_mm"], 1)
                if zero:
                    wait(pe, s_sum[0], p0)
                    wait(pe, s["value_hi"], n2)
                    wait(pe, s["value_lo"], n2)
                    rows_times(mid_ps, x0T, w_hop0, chunks=range(1), stop=False)
                if one:
                    aggregate(3 * p1 + 2, "gcn2")
                if two:
                    pe.wait_ge(s["queryT_hi"], n2)
                    pe.wait_ge(s["queryT_lo"], n2)
                    for c in range(C):
                        for i, (a, b) in enumerate(PASSES):
                            last = mm(scores_ps, query2T[:, a, c, :], x2T[:, b, c, :],
                                      start=c == 0 and i == 0, stop=c == C - 1 and i == 2)
                    last.then_inc(s["scores_mm"], 1)
                if one:
                    turn_relu(2 * p1 + 2)
                if zero:
                    rows_times(mid_ps, x0T, w_hop0, chunks=range(1, C), stop=False).then_inc(s["hop0_mm"], 1)
                if two:
                    pe.wait_ge(s["probs2"], n2)
                    wait(pe, s["trans0T_lo"], n0)
                    wait(pe, s["x3T_lo"], n3)
                    nc.tensor.transpose(turn_ps[:, 0:P], probs2[:], ident[:]).then_inc(s["probs2T_mm"], 1)
                if zero:
                    pe.wait_ge(s["y1_hi"], n0)
                    pe.wait_ge(s["y1_lo"], n0)
                    mix(mid_ps, high_low(trans0T), hop_y, start=False, stop=False)
                    add_bias(mid_ps, "hop").then_inc(s["hop_mm"], 1)
                if st.blocks_follow():
                    blocks_wait(pe, st)
                    wait(pe, s["queryT_lo"], n2)
                    wait(pe, s["y2_lo"], n0)
                    wait(pe, s["adjT_lo"], st.t)
                    for slot in range(2):
                        last = nc.tensor.transpose(adjT_ps[:, slot * P:(slot + 1) * P], adj_blocks[:, slot, :], ident[:])
                    last.then_inc(s["adjT_mm"], 1)
                if st.pair_follows():
                    wait(pe, s["probs2T_lo"], n2)
                    wait(pe, s["trans0T_lo"], n0)
                    wait(pe, s["x3T_lo"], n3)
                    turn_x0(st.t + 2)
                if two:
                    pe.wait_ge(s["probs2T_hi"], n2)
                    pe.wait_ge(s["probs2T_lo"], n2)
                    pe.wait_ge(s["value_lo"], n2)
                    wait(pe, s_sum[3], n3)
                    wait(pe, s_sum[2], p2)
                    mix(mix_ps, high_low(probs2T), value2).then_inc(s["mix_mm"], 1)
                if one:
                    support(3 * p1 + 3, w_gcn3)
                if st.pair_follows():
                    begin_hop1(st.t + 2)
                if one:
                    aggregate(3 * p1 + 3, None)

            turn_x0(1)
            begin_hop1(1)
            run_steps(pe, body)

        @block.scalar
        def _(act):
            def copy(dst, src):
                return nc.scalar.activation(dst, src, ACT.Copy)

            for i, w in enumerate(plain):
                slot, count = PLAIN_SLOT[i]
                act.wait_ge(s_slot[slot], count)
                copy(w[:, H, :, 0:D], raw[slot][:]).then_inc(s_plain_hi, 1)
            group = 0
            for dst in ([w_qk2[:, H, c, 0:D] for c in range(C)] + [None] * 3
                        + [w_v2[:, H, c, :] for c in range(C)] + [w_v3[:, H, c, 0:D] for c in range(C)]
                        + [w_v3[:, H, :, D:]]):
                group += 1
                if dst is None:
                    continue
                act.wait_ge(s_group, group)
                src = banks[(group - 1) % 8]
                if group == SETUP_GROUPS:
                    src = src.rearrange("p (c n) -> p c n", c=C)
                copy(dst, src).then_inc(s_group_hi, 1)
            act.wait_ge(s_setup_dve, 1)
            act.wait_ge(s_pool_lo, ON_POOL)

            def chunks(ps):
                return ps.rearrange("p (c n) -> p c n", c=C)

            def high(dst, src, ready, ready_count, done):
                act.wait_ge(ready, ready_count)
                copy(dst, src).then_inc(done, 1)

            def turn_x0(count):
                act.wait_ge(s["x0T_mm"], count)
                wait(act, s["hop0_mm"], count - 1)
                copy(x0T[:, H], chunks(turn_ps)).then_inc(s["x0T_hi"], 1)

            def feat_high(count):
                wait(act, s["support_mm"], count - 1)
                high(feat1[:, H], chunks(gcn_ps), s["turn1_mm"], count, s["feat_hi"])

            def node_high(count):
                wait(act, s["gcn_mm"], count - 1)
                high(node1[:, H], gcn_ps, s["support_mm"], count, s["node_hi"])

            def relu(count, gcn_count, turned, x0_read, turned_2):
                act.wait_ge(s["gcn_mm"], gcn_count)
                wait(act, s["turn1_mm"], turned)
                wait(act, s["x1_bias"], x0_read)
                wait(act, s["queryT_mm"], turned_2)
                nc.scalar.activation(relu1[:], gcn_ps, ACT.Relu).then_inc(s["relu1"], 1)

            def body(st):
                zero, one, two, three = (st.on(l) for l in range(LAYERS))
                n0, n1, n2, n3 = (st.now(l) for l in range(LAYERS))
                p0, p1, p2, p3 = (st.before(l) for l in range(LAYERS))
                if three:
                    wait(act, s["value3_mm"], p3)
                    high(x3T[:, H], chunks(turn_ps), s["x3T_mm"], n3, s["x3T_hi"])
                if one:
                    feat_high(3 * p1 + 1)
                if zero:
                    wait(act, s["hop_mm"], p0)
                    high(hop_y[:, H], wide_a[:, 0:D], s["hop2_mm"], n0, s["y2_hi"])
                if two:
                    wait(act, s["scores_mm"], p2)
                    high(x2T[:, H], chunks(mid_ps), s["x2T_mm"], n2, s["x2T_hi"])
                if one:
                    node_high(3 * p1 + 1)
                if zero:
                    act.wait_ge(s["edge_lrelu"], n0)
                    nc.scalar.activation(edge0[:], edge0[:], ACT.Exp).then_inc(s["edge_exp"], 1)
                if three:
                    wait(act, s["w3"], p3)
                    act.wait_ge(s["value3_mm"], n3)
                    copy(q3[:], wide_b[:, D:D + E3]).then_inc(s["q3"], 1)
                    wait(act, s["nbr3_mm"], p3)
                    copy(k3[:, H], wide_b[:, D + E3:]).then_inc(s["k3_hi"], 1)
                if one:
                    relu(2 * p1 + 1, 3 * p1 + 1, 3 * p1 + 1, n1, p2)
                if two:
                    wait(act, s["turn1_mm"], 3 * p1 + 2 if one else 3 * n1)
                    wait(act, s_x[0], p0)
                    wait(act, s["x1_bias"], n1)
                    high(query2[:], wide_a[:, 0:D], s["query_mm"], n2, s["query2"])
                if one:
                    feat_high(3 * p1 + 2)
                if zero:
                    wait(act, s["hop_mm"], p0)
                    high(trans0T[:, H], turn_ps[:, 0:P], s["trans0T_mm"], n0, s["trans0T_hi"])
                if two:
                    wait(act, s["mix_mm"], p2)
                    high(value2[:, H], mid_ps, s["value_mm"], n2, s["value_hi"])
                if three:
                    act.wait_ge(s["neg3"], n3)
                    nc.scalar.activation(work3[:], w3_bc_ps, ACT.Exp, bias=max3,
                                         accum_out=sum3).then_inc(s["exp3_all"], 1)
                    nc.scalar.activation(exp3, w3, ACT.Exp, bias=max3).then_inc(s["exp3"], 1)
                if one:
                    node_high(3 * p1 + 2)
                if two:
                    wait(act, s["scores_mm"], p2)
                    high(query2T[:, H], chunks(queryT_ps), s["queryT_mm"], n2, s["queryT_hi"])
                if zero:
                    high(hop_y[:, H], hop1_ps, s["hop12_mm"], n0, s["y1_hi"])
                if one:
                    relu(2 * p1 + 2, 3 * p1 + 2, 3 * p1 + 2, n1, n2)
                if two:
                    act.wait_ge(s["scores_mm"], n2)
                    act.wait_ge(s["rowbias2"], n2)
                    wait(act, s["probs2"], p2)
                    for g in HALVES:
                        last = nc.scalar.activation(attn2[g, :], scores_ps[g, g], ACT.Exp, bias=rowbias2[g, :])
                    last.then_inc(s["exp2"], 1)
                if one:
                    feat_high(3 * p1 + 3)
                if two:
                    wait(act, s["mix_mm"], p2)
                    high(probs2T[:, H], turn_ps[:, 0:P], s["probs2T_mm"], n2, s["probs2T_hi"])
                if st.pair_follows():
                    turn_x0(st.t + 2)
                if one:
                    node_high(3 * p1 + 3)
                if st.blocks_follow():
                    wait(act, s["gcn_mm"], 3 * n1)
                    wait(act, s["nbr3_mm"], n3)
                    act.wait_ge(s["adjT_mm"], st.t + 1)
                    copy(adjT[:, H], adjT_ps.rearrange("p (a n) -> p a n", a=2)).then_inc(s["adjT_hi"], 1)

            turn_x0(1)
            run_steps(act, body)

        @block.vector
        def _(dve):
            setup_step = [0]

            def link(ins):
                setup_step[0] += 1
                ins.then_inc(s_dve_setup, 1)
                dve.wait_ge(s_dve_setup, setup_step[0])

            ve = nc.vector
            ve.memset(ones[:], 1.0)
            ve.memset(bq_wide[:], 0.0)
            ve.memset(same_graph[:], 0.0)
            link(ve.memset(row_raw[:], 0.0))
            for g in HALVES:
                ve.memset(same_graph[g, g], 1.0)
            dve.wait_ge(s_vec_loaded, 16 * 12)
            dve.wait_ge(s_pool_const, 3)
            for r in range(2):
                ve.tensor_copy(bq_wide[:, :, KEY_ROW + r:KEY_ROW + r + 1], bq_col[:].rearrange("p (c a) -> p c a", a=1))
            link(ve.tensor_tensor_reduce(out=junk[:, 0:C], in0=bq_col[:], in1=bk_col[:], scale=1.0, scalar=0.0,
                                         op0=ALU.mult, op1=ALU.add, accum_out=sums[:, 0:1]))
            ve.tensor_tensor(node_ident[:], ident[:, 0:N], ident[:, N:P], ALU.add).then_inc(s_small_ready, 1)
            ve.tensor_reduce(even, ident[:, 0::2], AX.X, ALU.add)
            ve.tensor_reduce(odd, ident[:, 1::2], AX.X, ALU.add)
            for i, (a, b) in enumerate(BIAS_ROWS.values()):
                last = ve.tensor_reduce(pick[:, i:i + 1], ident[:, a:b], AX.X, ALU.add)
            link(last)
            for i, n in enumerate(BIAS_ROWS):
                ve.tensor_scalar(select[n][:], ones[:], pick[:, i:i + 1], None, ALU.mult)
            for a in range(2):
                last = ve.tensor_tensor_reduce(out=junk, in0=bv_all[:], in1=aw_all[:, a, :], scale=1.0, scalar=0.0,
                                               op0=ALU.mult, op1=ALU.add, accum_out=sums[:, 1 + a:2 + a])
                link(last)
            dve.wait_ge(s_slot[2], 16)
            for c in range(C):
                for a in range(2):
                    link(ve.tensor_tensor_reduce(out=junk, in0=raw[2][:, c, :], in1=aw_all[:, a, :], scale=1.0,
                                                 scalar=0.0, op0=ALU.mult, op1=ALU.add,
                                                 accum_out=edge_raw[:, c, a:a + 1]))
            link(ve.tensor_copy(w_hop2[:, H, :, D:], edge_raw[:]))
            ve.tensor_tensor(w_hop2[:, L, :, D:], edge_raw[:], w_hop2[:, H, :, D:].bitcast(F32), ALU.subtract) \
                .then_inc(s_edge_used, 1)
            link(ve.tensor_tensor(edge_const, sums[:, 1:2], sums[:, 2:3], ALU.add))
            link(ve.tensor_tensor(edge_const, edge_const, ab_all[:], ALU.add))
            for i, w in enumerate(plain[:-ON_POOL]):
                dve.wait_ge(s_plain_hi, i + 1)
                slot = PLAIN_SLOT[i][0]
                ve.tensor_tensor(w[:, L, :, 0:D], raw[slot][:], w[:, H, :, 0:D].bitcast(F32), ALU.subtract) \
                    .then_inc(s_plain_lo, 1)
            highs = 0
            for group, w in enumerate([(w_qk2, c) for c in range(C)] + [None] * 3
                                      + [(w_v2, c) for c in range(C)] + [(w_v3, c) for c in range(C)]
                                      + [(w_v3, None)]):
                src = banks[group % 8]
                if w:
                    highs += 1
                    dve.wait_ge(s_group_hi, highs)
                    m, c = w
                    if c is None:
                        ve.tensor_tensor(m[:, L, :, D:], src.rearrange("p (c n) -> p c n", c=C),
                                         m[:, H, :, D:].bitcast(F32), ALU.subtract).then_inc(s_group_out, 1)
                    else:
                        ve.tensor_tensor(m[:, L, c, 0:D], src, m[:, H, c, 0:D].bitcast(F32), ALU.subtract) \
                            .then_inc(s_group_out, 1)
                    continue
                dve.wait_ge(s_group, group + 1)
                if group == C:
                    ve.tensor_tensor(bias_raw[0:16, :], bias_raw[0:16, :], src[0:16, :], ALU.add) \
                        .then_inc(s_group_out, 1)
                    dve.wait_ge(s_group_out, group + 1)
                    link(ve.tensor_copy(bias_rows[:], bias_raw[:]))
                    link(ve.tensor_tensor(bias_raw[:], bias_raw[:], bias_rows[:].bitcast(F32), ALU.subtract))
                    link(ve.tensor_scalar(bias_raw[:], bias_raw[:], odd, None, ALU.mult))
                    link(ve.scalar_tensor_tensor(out=bias_rows[:], in0=bias_rows[:].bitcast(F32), scalar=even,
                                                 in1=bias_raw[:], op0=ALU.mult, op1=ALU.add))
                elif group == C + 1:
                    ve.tensor_copy(row_raw[:, :, 0:1], src[:, 0:C].rearrange("p (c a) -> p c a", a=1)) \
                        .then_inc(s_group_out, 1)
                    dve.wait_ge(s_group_out, group + 1)
                    link(ve.tensor_copy(w_qk2[:, H, :, D:], row_raw[:]))
                    link(ve.tensor_tensor(w_qk2[:, L, :, D:], row_raw[:], w_qk2[:, H, :, D:].bitcast(F32),
                                          ALU.subtract))
                else:
                    ve.tensor_copy(row_const, src[:, 0:1]).then_inc(s_group_out, 1)
            dve.wait_ge(s_group_out, SETUP_GROUPS)
            link(ve.memset(sums[:], 0.0))
            ve.memset(pad, 0.0).then_inc(s_setup_dve, 1)
            dve.wait_ge(s_pool_lo, ON_POOL)

            def chunks(ps):
                return ps.rearrange("p (c n) -> p c n", c=C)

            def low(dst, src, high, hi_done, hi_count, done):
                dve.wait_ge(hi_done, hi_count)
                ve.tensor_tensor(dst, src, high.bitcast(F32), ALU.subtract).then_inc(done, 1)

            def feat_low(count):
                low(feat1[:, L], chunks(gcn_ps), feat1[:, H], s["feat_hi"], count, s["feat_lo"])

            def node_low(count):
                low(node1[:, L], gcn_ps, node1[:, H], s["node_hi"], count, s["node_lo"])

            def diagonal_blocks(dst, src, scale, done):
                for g in HALVES:
                    last = ve.tensor_scalar(dst[g, g], src[g, :], scale[g, :], None, ALU.mult)
                last.then_inc(done, 1)

            def statistics(l, count):
                dve.wait_ge(s_sum[l], count)
                ve.bn_stats(stats[l], sum_of[l][:]).then_inc(s_stats[l], 1)

            def moments_of(l):
                ve.bn_aggr(moments[l], stats[l]).then_inc(s_moments[l], 1)

            def add_eps(l, count):
                dve.wait_ge(s_moments[l], count)
                ve.tensor_scalar(var_eps[l], moments[l][:, 1:2], LN_EPS, None, ALU.add).then_inc(s_vareps[l], 1)

            def normalise(l, count):
                dve.wait_ge(s_rstd[l], count)
                ve.tensor_scalar(sum_of[l][:], sum_of[l][:], moments[l][:, 0:1], rstd[l], ALU.subtract, ALU.mult) \
                    .then_inc(s_x[l], 1)

            def turn_x0(count):
                wait(dve, s["hop0_mm"], count - 1)
                low(x0T[:, L], chunks(turn_ps), x0T[:, H], s["x0T_hi"], count, s["x0T_lo"])

            def body(st):
                zero, one, two, three = (st.on(l) for l in range(LAYERS))
                n0, n1, n2, n3 = (st.now(l) for l in range(LAYERS))
                p0, p1, p2, p3 = (st.before(l) for l in range(LAYERS))
                if one:
                    feat_low(3 * p1 + 1)
                if three:
                    low(x3T[:, L], chunks(turn_ps), x3T[:, H], s["x3T_hi"], n3, s["x3T_lo"])
                if zero:
                    low(hop_y[:, L], wide_a[:, 0:D], hop_y[:, H], s["y2_hi"], n0, s["y2_lo"])
                    wait(dve, s["edge_bc_mm"], p0)
                    wait(dve, s["w3_bc_mm"], p3)
                    ve.tensor_scalar(diag0[:], node_ident[:], wide_a[:, D:D + 1], None, ALU.mult) \
                        .then_inc(s["diag0"], 1)
                    ve.tensor_tensor(edge_i, wide_a[:, D + 1:D + 2], edge_const, ALU.add).then_inc(s["edge_i"], 1)
                if two:
                    low(x2T[:, L], chunks(mid_ps), x2T[:, H], s["x2T_hi"], n2, s["x2T_lo"])
                if one:
                    node_low(3 * p1 + 1)
                if zero:
                    dve.wait_ge(s["edge_bc_mm"], n0)
                    dve.wait_ge(s["edge_i"], n0)
                    wait(dve, s["exp3_all"], p3)
                    ve.tensor_scalar(edge0[:], edge_bc_ps, edge_i, None, ALU.add).then_inc(s["edge_sum"], 1)
                    dve.wait_ge(s["edge_sum"], n0)
                    ve.scalar_tensor_tensor(out=edge0[:], in0=edge0[:], scalar=SLOPE, in1=edge0[:], op0=ALU.mult,
                                            op1=ALU.max).then_inc(s["edge_lrelu"], 1)
                    dve.wait_ge(s["edge_exp"], n0)
                    dve.wait_ge(s["adj0_loaded"], 16 * n0)
                    ve.tensor_tensor_reduce(out=edge0[:], in0=edge0[:], in1=adj0[:], scale=1.0, scalar=0.0,
                                            op0=ALU.mult, op1=ALU.add, accum_out=rowsum0).then_inc(s["alpha0"], 1)
                    dve.wait_ge(s["alpha0"], n0)
                    ve.tensor_scalar(rowsum0, rowsum0, ROWSUM_EPS, None, ALU.add).then_inc(s["den0"], 1)
                    dve.wait_ge(s["den0"], n0)
                    ve.reciprocal(inv0, rowsum0).then_inc(s["inv0"], 1)
                    dve.wait_ge(s["inv0"], n0)
                    wait(dve, s["trans0T_mm"], p0)
                    diagonal_blocks(trans0, edge0, inv0, s["trans0"])
                if three:
                    low(k3[:, L], wide_b[:, D + E3:], k3[:, H], s["k3_hi"], n3, s["k3_lo"])
                if two:
                    dve.wait_ge(s["query_mm"], n2)
                    dve.wait_ge(s["query2"], n2)
                    wait(dve, s["exp2"], p2)
                    ve.tensor_tensor(rowbias2, wide_a[:, D:D + 1], row_const, ALU.add).then_inc(s["rowbias2"], 1)
                if one:
                    feat_low(3 * p1 + 2)
                if three:
                    dve.wait_ge(s["nbr3_mm"], n3)
                    dve.wait_ge(s["q3"], n3)
                    wait(dve, s["trans0"], n0)
                    wait(dve, s["exp3_all"], p3)
                    wait(dve, s["exp3"], p3)
                    ve.tensor_tensor_reduce(out=work3[:], in0=q3[:], in1=nbr3_ps, scale=SCALE3, scalar=0.0,
                                            op0=ALU.mult, op1=ALU.add, accum_out=w3).then_inc(s["w3"], 1)
                    dve.wait_ge(s["w3"], n3)
                    wait(dve, s["w3_bc_mm"], p3)
                    wait(dve, s["edge_bc_mm"], n0)
                    ve.tensor_scalar(diag3[:], node_ident[:], w3, None, ALU.mult).then_inc(s["diag3"], 1)
                if zero:
                    low(trans0T[:, L], turn_ps[:, 0:P], trans0T[:, H], s["trans0T_hi"], n0, s["trans0T_lo"])
                if two:
                    low(value2[:, L], mid_ps, value2[:, H], s["value_hi"], n2, s["value_lo"])
                if three:
                    dve.wait_ge(s["w3_bc_mm"], n3)
                    ve.reduce_max(max3, w3_bc_ps, AX.X).then_inc(s["max3"], 1)
                    dve.wait_ge(s["max3"], n3)
                    ve.tensor_scalar(max3, max3, -1.0, None, ALU.mult).then_inc(s["neg3"], 1)
                if one:
                    node_low(3 * p1 + 2)
                if two:
                    low(query2T[:, L], chunks(queryT_ps), query2T[:, H], s["queryT_hi"], n2, s["queryT_lo"])
                if zero:
                    low(hop_y[:, L], hop1_ps, hop_y[:, H], s["y1_hi"], n0, s["y1_lo"])
                if three:
                    dve.wait_ge(s["exp3_all"], n3)
                    ve.reciprocal(inv3, sum3).then_inc(s["inv3"], 1)
                    dve.wait_ge(s["inv3"], n3)
                    dve.wait_ge(s["exp3"], n3)
                    ve.tensor_tensor(gate3, exp3, inv3, ALU.mult).then_inc(s["gate3"], 1)
                if three:
                    dve.wait_ge(s["gate3"], n3)
                    dve.wait_ge(s["value3_mm"], n3)
                    ve.scalar_tensor_tensor(out=x3[:], in0=wide_b[:, 0:D], scalar=gate3, in1=x3[:], op0=ALU.mult,
                                            op1=ALU.add).then_inc(s_sum[3], 1)
                    statistics(3, n3)
                if two:
                    dve.wait_ge(s["exp2"], n2)
                    dve.wait_ge(s["adj2_loaded"], 16 * n2)
                    if three:
                        dve.wait_ge(s_stats[3], n3)
                    ve.tensor_tensor_reduce(out=attn2[:], in0=attn2[:], in1=adj2[:], scale=1.0, scalar=0.0,
                                            op0=ALU.mult, op1=ALU.add, accum_out=rowsum2).then_inc(s["attn2"], 1)
                if three:
                    if not two:
                        dve.wait_ge(s_stats[3], n3)
                    moments_of(3)
                    add_eps(3, n3)
                if two:
                    dve.wait_ge(s["attn2"], n2)
                    ve.reciprocal(inv2, rowsum2).then_inc(s["inv2"], 1)
                    dve.wait_ge(s["inv2"], n2)
                    wait(dve, s["probs2T_mm"], p2)
                    diagonal_blocks(probs2, attn2, inv2, s["probs2"])
                if three:
                    normalise(3, n3)
                if one:
                    feat_low(3 * p1 + 3)
                if two:
                    low(probs2T[:, L], turn_ps[:, 0:P], probs2T[:, H], s["probs2T_hi"], n2, s["probs2T_lo"])
                if st.pair_follows():
                    turn_x0(st.t + 2)
                if zero:
                    dve.wait_ge(s["hop_mm"], n0)
                    dve.wait_ge(s["res_loaded"], 16 * n0)
                    ve.scalar_tensor_tensor(out=x0_res[:], in0=mid_ps, scalar=0.0, in1=x0_res[:], op0=ALU.max,
                                            op1=ALU.add).then_inc(s_sum[0], 1)
                    statistics(0, n0)
                if two:
                    dve.wait_ge(s["mix_mm"], n2)
                    dve.wait_ge(s["x2_bias"], n2)
                    wait(dve, s["out_stored"], 16 * n3)
                    ve.tensor_tensor(x3[:], mix_ps, x2[:], ALU.add).then_inc(s_sum[2], 1)
                    statistics(2, n2)
                    dve.wait_ge(s_stats[2], n2)
                if zero:
                    dve.wait_ge(s_stats[0], n0)
                if one:
                    node_low(3 * p1 + 3)
                if two:
                    moments_of(2)
                if zero:
                    moments_of(0)
                if two:
                    add_eps(2, n2)
                if zero:
                    add_eps(0, n0)
                if two:
                    normalise(2, n2)
                if zero:
                    normalise(0, n0)
                if one:
                    dve.wait_ge(s["gcn_mm"], 3 * n1)
                    dve.wait_ge(s["x1_bias"], n1)
                    wait(dve, s_sum[2], n2)
                    ve.tensor_tensor(x2[:], gcn_ps, x1[:], ALU.add).then_inc(s_sum[1], 1)
                if st.blocks_follow():
                    low(adjT[:, L], adjT_ps.rearrange("p (a n) -> p a n", a=2), adjT[:, H],
                        s["adjT_hi"], st.t + 1, s["adjT_lo"])
                if one:
                    statistics(1, n1)
                    dve.wait_ge(s_stats[1], n1)
                    ve.memset(pad, 0.0)
                    moments_of(1)
                    add_eps(1, n1)
                    normalise(1, n1)

            turn_x0(1)
            run_steps(dve, body)


_INS = ['x', 'adj', 'L0_gnn_Wv', 'L0_gnn_bv', 'L0_gnn_aw', 'L0_gnn_ab', 'L0_gnn_Wk', 'L0_gnn_bk',
        'L1_gnn_W1', 'L1_gnn_b1', 'L1_gnn_W2', 'L1_gnn_b2', 'L1_gnn_W3', 'L1_gnn_b3',
        'L2_gnn_Wq_w', 'L2_gnn_Wq_b', 'L2_gnn_Wk_w', 'L2_gnn_Wk_b', 'L2_gnn_Wv_w', 'L2_gnn_Wv_b',
        'L3_gnn_W_qk', 'L3_gnn_W_v']


def kernel(**inputs):
    import numpy as _np
    import concourse.bacc as _bacc
    from concourse import mybir as _mybir
    from concourse.bass_utils import run_bass_kernel_spmd as _run

    nc = _bacc.Bacc("TRN2", target_bir_lowering=False, num_devices=1)
    arrays, args = {}, []
    for name in _INS:
        a = _np.ascontiguousarray(inputs[name])
        arrays[f"in_{name}_dram"] = a
        args.append(nc.dram_tensor(f"in_{name}_dram", a.shape, _mybir.dt.from_np(a.dtype), kind="ExternalInput").ap())
    args.append(nc.dram_tensor("out_0_dram", inputs["x"].shape, _mybir.dt.float32, kind="ExternalOutput").ap())
    build(nc, *args)
    r = _run(nc, [arrays], core_ids=[0])
    return r.results[0]["out_0_dram"]
```

```python
from contextlib import ExitStack

import concourse.bass as bass
from concourse import mybir

F32 = mybir.dt.float32
F32R = mybir.dt.float32r
ALU = mybir.AluOpType
ACT = mybir.ActivationFunctionType
AX = mybir.AxisListType

H, L = 0, 1
PASSES = ((H, H), (H, L), (L, H))
P = 128
LAYERS = 4
LN_EPS = 1e-5
ROWSUM_EPS = 1e-12
SLOPE = 0.2


def wait(eng, sem, count):
    if isinstance(count, int) and count <= 0:
        return
    eng.wait_ge(sem, count)


def build(nc, x, adj, Wv0, bv0, aw0, ab0, Wk0, bk0, W1, b1, W2, b2, W3, b3,
          Wq2, bq2, Wk2, bk2, Wv2, bv2, Wqk3, Wv3, out):
    graphs, N, D = x.shape
    C = D // P
    PAIRS = graphs * N // P
    E3 = Wqk3.shape[0] // 2
    SCALE3 = float(E3) ** -0.5
    HALVES = (slice(0, N), slice(N, P))
    assert 2 * N == P and D == 512 and 2 * E3 == P and PAIRS > 2 * LAYERS - 2

    x_pairs = x.rearrange("(t g) n d -> t (g n) d", g=2)
    out_pairs = out.rearrange("(t g) n d -> t (g n) d", g=2)
    adj_pairs = adj.rearrange("(t g) i j -> t (g i) j", g=2)
    adj_graphs = adj.rearrange("(t g) i j -> t g i j", g=2)

    with ExitStack() as ctx:
        def sb(name, shape, dt=F32):
            return ctx.enter_context(nc.sbuf_tensor(name, shape, dt))

        def sem(name):
            return ctx.enter_context(nc.semaphore(name))

        EDGE = ROW = 2
        w_hop1 = sb("w_hop1", [P, 2, C, D], F32R)
        w_hop2 = sb("w_hop2", [P, 2, C, D + EDGE], F32R)
        w_hop0 = sb("w_hop0", [P, 2, C, D], F32R)
        w_gcn1 = sb("w_gcn1", [P, 2, C, D], F32R)
        w_gcn2 = sb("w_gcn2", [P, 2, C, D], F32R)
        w_gcn3 = sb("w_gcn3", [P, 2, C, D], F32R)
        plain = [w_hop1, w_hop2, w_hop0, w_gcn1, w_gcn2, w_gcn3]
        w_qk2 = sb("w_qk2", [P, 2, C, D + ROW], F32R)
        with ExitStack() as early:
            def small(name, shape):
                return early.enter_context(nc.sbuf_tensor(name, shape, F32))

            ones = small("ones", [P, P])
            bq_col = small("bq_col", [P, C])
            bk_col = small("bk_col", [P, C])
            bq_wide = small("bq_wide", [P, C, P])
            edge_raw = small("edge_raw", [P, C, 2])
            row_raw = small("row_raw", [P, C, 2])
            ab_all = small("ab_all", [P, 1])
            sums = small("sums", [P, 3])
            qk3_raw = small("qk3_raw", [P, D])
            aw_all, bv_all, *bias_hops = (early.enter_context(nc.sbuf_tensor(n, [P, w, D], F32)) for n, w in
                                          (("aw_all", 2), ("bv_all", 1), ("bias_hop1", 1), ("bias_hop2", 1)))
        w_v2 = sb("w_v2", [P, 2, C, D], F32R)
        w_v3 = sb("w_v3", [P, 2, C, D + 2 * E3], F32R)
        ident = sb("ident", [P, P])
        same_graph = sb("same_graph", [P, P])
        node_ident = sb("node_ident", [P, N])
        bias_hop, bias_gcn1, bias_gcn2, bias_gcn3, bias_key2, bias_v2 = (
            sb(f"bias_{n}", [P, D]) for n in ("hop", "gcn1", "gcn2", "gcn3", "key2", "v2"))
        cols = sb("cols", [P, 96])
        used_cols = [0]

        def col(n=1):
            used_cols[0] += n
            return cols[:, used_cols[0] - n:used_cols[0]]

        edge_const = col()
        row_const = col()
        minus_half = col()
        pad, pad0 = col(), col()

        x0_in = sb("x0_in", [P, D])

        SLOTS = 5
        raw = [None] * SLOTS
        with ExitStack() as staging:
            for i in range(2, SLOTS):
                raw[i] = staging.enter_context(nc.sbuf_tensor(f"raw{i}", [P, C, D], F32))
        hop_y = sb("hop_y", [P, 2, D], F32R)
        work3 = sb("work3", [P, 2, N])
        edge0, diag0 = work3[:, 0, :], work3[:, 1, :]
        diag3 = diag0
        trans0 = sb("trans0", [P, P])
        trans0T = sb("trans0T", [P, 2, P], F32R)
        x1 = sb("x1", [P, D])
        x0_res = sb("x0_res", [P, D])
        hidden1 = query2 = x0_res
        node1 = sb("node1", [P, 2, D], F32R)
        feat1 = sb("feat1", [P, 2, C, P], F32R)
        adj_blocks = sb("adj_blocks", [P, 2, P])
        adjT = sb("adjT", [P, 2, 2, P], F32R)
        x2 = sb("x2", [P, D])
        adj2 = sb("adj2", [P, N])
        probs2 = sb("probs2", [P, P])
        adj0 = sb("adj0", [P, N])
        x0T = sb("x0T", [P, 2, C, P], F32R)
        with ExitStack() as staging:
            for i in range(2):
                raw[i] = staging.enter_context(nc.sbuf_tensor(f"raw{i}", [P, C, D], F32))
        x2T = sb("x2T", [P, 2, C, P], F32R)
        value2 = sb("value2", [P, 2, D], F32R)
        attn2 = sb("attn2", [P, N])
        probs2T = sb("probs2T", [P, 2, P], F32R)
        x3 = sb("x3", [P, D])
        x3T = sb("x3T", [P, 2, C, P], F32R)
        query2T = x3T
        q3 = sb("q3", [P, E3])
        k3 = sb("k3", [P, 2, E3], F32R)
        sum_of = [x0_res, x1, x2, x3]
        norm_of = [x0_res, x2, x3, x0_in]
        edge_i = col()
        rowsum0, inv0 = col(), col()
        rowbias2 = col()
        rowsum2, inv2 = col(), col()
        w3, max3, exp3, sum3, inv3, gate3 = col(), col(), col(), col(), col(), col()
        stats = [col(6) for _ in range(LAYERS)]
        moments = [col(2) for _ in range(LAYERS)]
        var_eps = [col() for _ in range(LAYERS)]
        rstd = [col() for _ in range(LAYERS)]
        shift = {l: col() for l in (0, 3)}

        M_GROUPS, KEY_BIAS, ROW_WEIGHTS, ROW_CONST, QK3 = C, C, C + 1, C + 2, C + 3
        SETUP_GROUPS = QK3 + 1
        ALL_GROUPS = SETUP_GROUPS + 2 * C

        BANK = 512
        bank = [ctx.enter_context(nc.psum_tensor(f"bank{i}", [P, BANK], F32)) for i in range(4)]
        pair_a = ctx.enter_context(nc.psum_tensor("pair_a", [P, 2 * BANK], F32))
        pair_b = ctx.enter_context(nc.psum_tensor("pair_b", [P, 2 * BANK], F32))
        hop1_ps, mid_ps, turn_ps, gcn_ps = (b[:] for b in bank)
        banks = [b[:] for b in bank] + [pair_a[:, 0:BANK], pair_a[:, BANK:], pair_b[:, 0:BANK], pair_b[:, BANK:]]
        LEAD_A, LEAD_B = D // 2, (D + 2 * E3) // 2
        junk = pair_b[:, BANK:]
        wide_a = pair_a[:, BANK - LEAD_A:BANK - LEAD_A + D + EDGE]
        wide_b = pair_b[:, BANK - LEAD_B:BANK - LEAD_B + D + 2 * E3]
        edge_bc_ps = pair_a[:, BANK:BANK + N]
        adjT_ps = pair_a[:, 0:2 * P]
        queryT_ps = pair_a[:, 0:BANK]
        scores_ps = pair_a[:, BANK:BANK + 2 * P].rearrange("p (a n) -> p a n", a=2)
        mix_ps = pair_b[:, 0:BANK]
        nbr3_ps = pair_b[:, 2 * BANK - 3 * N:2 * BANK - N].rearrange("p (a n) -> p a n", a=2)
        w3_bc_ps = pair_b[:, 2 * BANK - N:2 * BANK]

        s_slot = [sem(f"slot{i}") for i in range(SLOTS)]
        s_qk3_loaded = sem("qk3_loaded")
        s_vec_loaded = sem("vec_loaded")
        VECTORS = 6
        s_bias_loaded = sem("bias_loaded")
        BIASES = 7
        s_pool_const = sem("pool_const")
        s_pool_lo = sem("pool_lo")
        s_dve_setup = sem("dve_setup")
        PLAIN_SLOT = ((3, 16), (4, 16), (2, 32), (3, 32), (4, 32), (2, 48))
        ON_POOL = 3
        s_plain_hi = sem("plain_hi")
        s_plain_lo = sem("plain_lo")
        s_edge_used = sem("edge_used")
        s_small_ready = sem("small_ready")
        s_group = sem("setup_group")
        s_group_hi = sem("setup_group_hi")
        s_group_out = sem("setup_group_out")
        s_setup_dve = sem("setup_dve_done")

        names = """
            x0_loaded res_loaded adj0_loaded blocks_loaded adj2_loaded out_stored
            x0T_mm x0T_hi x0T_lo hop2_mm diag0 edge_i edge_bc_mm edge_sum edge_lrelu edge_exp
            alpha0 den0 inv0 trans0 trans0T_mm trans0T_hi trans0T_lo y2_hi y2_lo
            hop12_mm y1_hi y1_lo hop0_mm hop_mm hop_bias
            adjT_mm adjT_hi adjT_lo x1_bias x2_bias turn1_mm feat_hi feat_lo support_mm node_hi node_lo gcn_mm hidden1
            x2T_mm x2T_hi x2T_lo query_mm query2 queryT_mm queryT_hi queryT_lo value_mm value_hi value_lo
            scores_mm rowbias2 scores2 exp2 attn2 inv2 probs2 probs2T_mm probs2T_hi probs2T_lo mix_mm
            x3T_mm x3T_hi x3T_lo qk3_mm value3_mm q3 k3_hi k3_lo nbr3_mm w3 diag3 w3_bc_mm
            max3 neg3 exp3_all exp3 inv3 gate3
        """.split()
        s = {n: sem(n) for n in names}
        s_sum = [sem(f"sum{l}") for l in range(LAYERS)]
        s_stats = [sem(f"stats{l}") for l in range(LAYERS)]
        s_moments = [sem(f"moments{l}") for l in range(LAYERS)]
        s_vareps = [sem(f"vareps{l}") for l in range(LAYERS)]
        s_rstd = [sem(f"rstd{l}") for l in range(LAYERS)]
        s_shift = {l: sem(f"shift{l}") for l in shift}
        s_x = [sem(f"x{l + 1}") for l in range(LAYERS)]

        def setup_bank(group):
            return banks[group if group < SETUP_GROUPS else 6 + group % 2]

        def made_v(k):
            return (w_v2, w_v3)[k // C], k % C

        class Step:

            def __init__(self, t):
                self.t = t

            def on(self, layer):
                return not isinstance(self.t, int) or 0 <= self.t - layer < PAIRS

            def now(self, layer):
                n = self.t - layer + 1
                return max(0, min(n, PAIRS)) if isinstance(n, int) else n

            def before(self, layer):
                n = self.t - layer
                return max(0, min(n, PAIRS)) if isinstance(n, int) else n

            def is_step(self, t):
                return isinstance(self.t, int) and self.t == t

            def pair_follows(self):
                return not isinstance(self.t, int) or self.t < PAIRS - 1

            def blocks_follow(self):
                return not isinstance(self.t, int) or self.t < PAIRS + LAYERS - 2

        def run_steps(eng, body):
            for t in range(LAYERS):
                body(Step(t))
            with eng.Fori(LAYERS, PAIRS - 1) as t:
                body(Step(t))
            for t in range(PAIRS - 1, PAIRS + LAYERS - 1):
                body(Step(t))

        block = ctx.enter_context(nc.Block())

        @block.sync
        def _(sp):
            sp.dma_start(bq_col[:], bq2.rearrange("(c p) -> p c", p=P), allow_slow_non_contiguous=True) \
                .then_inc(s_vec_loaded, 16)
            sp.dma_start(bk_col[:], bk2.rearrange("(c p) -> p c", p=P), allow_slow_non_contiguous=True) \
                .then_inc(s_vec_loaded, 16)

            def load(i):
                w, slot, free, count = matrices[i]
                if free is not None:
                    sp.wait_ge(free, count)
                sp.dma_start(raw[slot][:], w.rearrange("(c p) n -> p c n", p=P)).then_inc(s_slot[slot], 16)

            matrices = [(Wq2, 0, None, 0), (Wk2, 1, None, 0), (Wv0, 2, None, 0), (Wk0[1], 3, None, 0),
                        (Wk0[2], 4, None, 0), (Wk0[0], 2, s_edge_used, 1), (W1, 3, s_plain_lo, 1),
                        (W2, 4, s_plain_lo, 2), (W3, 2, s_plain_lo, 3),
                        (Wv2, 0, s_group, ROW_WEIGHTS + 1), (Wv3, 1, s_group, ROW_WEIGHTS + 1)]
            load(0)
            load(1)

            def row(v):
                return v.rearrange("(a n) -> a n", a=1)

            for i in range(2):
                sp.dma_start(aw_all[:, i, :], aw0[i * D:(i + 1) * D].rearrange("n b -> b n").broadcast_to([P, D])) \
                    .then_inc(s_vec_loaded, 16)
            sp.dma_start(bv_all[:, 0, :], row(bv0).broadcast_to([P, D])).then_inc(s_vec_loaded, 16)
            sp.dma_start(ab_all[:], row(ab0).broadcast_to([P, 1])).then_inc(s_vec_loaded, 16)
            load(2)
            load(3)
            for dst, b in ((bias_hop[:], bk0[0]), (bias_hops[0][:, 0, :], bk0[1]), (bias_hops[1][:, 0, :], bk0[2]),
                           (bias_gcn1[:], b1), (bias_gcn2[:], b2), (bias_gcn3[:], b3), (bias_v2[:], bv2)):
                sp.dma_start(dst, row(b).broadcast_to([P, D])).then_inc(s_bias_loaded, 16)
            sp.dma_start(qk3_raw[:], Wqk3).then_inc(s_qk3_loaded, 16)
            sp.dma_start(x0_in[:], x_pairs[0]).then_inc(s["x0_loaded"], 16)
            for i in range(4, len(matrices)):
                load(i)

            sp.wait_ge(s_setup_dve, 1)
            sp.wait_ge(s_pool_lo, 1)
            sp.wait_ge(s_group, SETUP_GROUPS)
            sp.dma_start(adj0[:], adj_pairs[0]).then_inc(s["adj0_loaded"], 16)
            sp.wait_ge(s_pool_const, 3)

            def body(st):
                t = st.t
                nxt = Step(t + 1)
                if st.blocks_follow():
                    wait(sp, s["adjT_mm"], t)
                    for slot, layer in ((0, 1), (1, 3)):
                        if nxt.on(layer):
                            for g in range(2):
                                sp.dma_start(adj_blocks[HALVES[g], slot, HALVES[g]],
                                             adj_graphs[t + 1 - layer, g]).then_inc(s["blocks_loaded"], 16)
                if st.pair_follows():
                    wait(sp, s["x0T_mm"], st.now(0))
                    wait(sp, s["out_stored"], 16 * st.before(3))
                    sp.dma_start(x0_in[:], x_pairs[t + 1]).then_inc(s["x0_loaded"], 16)
                    wait(sp, s["alpha0"], st.now(0))
                    sp.dma_start(adj0[:], adj_pairs[t + 1]).then_inc(s["adj0_loaded"], 16)
                if nxt.on(2):
                    wait(sp, s["attn2"], st.now(2))
                    sp.dma_start(adj2[:], adj_pairs[t - 1]).then_inc(s["adj2_loaded"], 16)
                if st.on(0):
                    wait(sp, s["turn1_mm"], 3 * st.now(1))
                    wait(sp, s["x1_bias"], st.now(1))
                    wait(sp, s["queryT_mm"], st.now(2))
                    sp.dma_start(x0_res[:], x_pairs[t]).then_inc(s["res_loaded"], 16)
                if st.on(3):
                    sp.wait_ge(s_x[3], st.now(3))
                    sp.dma_start(out_pairs[t - 3], norm_of[3][:]).then_inc(s["out_stored"], 16)

            run_steps(sp, body)
            sp.wait_ge(s["out_stored"], 16 * PAIRS)

        @block.gpsimd
        def _(pool):
            nc.gpsimd.memset(ident[:], 0.0).then_inc(s_pool_const, 1)
            pool.wait_ge(s_pool_const, 1)
            nc.gpsimd.affine_select(out=ident[:], in_=ident[:], compare_op=ALU.not_equal, fill=1.0,
                                    base=0, pattern=[[-1, P]], channel_multiplier=1).then_inc(s_pool_const, 1)
            nc.gpsimd.memset(minus_half, -0.5)
            pool.wait_ge(s_plain_hi, ON_POOL + 1)
            nc.gpsimd.tensor_tensor(plain[ON_POOL][:, L, :, 0:D], raw[PLAIN_SLOT[ON_POOL][0]][:],
                                    plain[ON_POOL][:, H, :, 0:D].bitcast(F32), ALU.subtract).then_inc(s_pool_lo, 1)
            pool.wait_ge(s_setup_dve, 1)
            pool.wait_ge(s_pool_lo, 1)
            pool.wait_ge(s_group, SETUP_GROUPS)
            nc.gpsimd.memset(trans0[:], 0.0)
            nc.gpsimd.memset(probs2[:], 0.0)
            nc.gpsimd.memset(adj_blocks[:], 0.0).then_inc(s_pool_const, 1)
            pool.wait_ge(s_bias_loaded, 16 * BIASES)

            def inv_std(layer, count):
                pool.wait_ge(s_vareps[layer], count)
                nc.gpsimd.tensor_tensor(rstd[layer], var_eps[layer], minus_half, ALU.pow).then_inc(s_rstd[layer], 1)

            def body(st):
                n0, n1, n2, n3 = (st.now(l) for l in range(LAYERS))
                if st.on(1):
                    pool.wait_ge(s_x[0], n1)
                    wait(pool, s_x[1], st.before(1))
                    nc.gpsimd.tensor_tensor(x1[:], x0_res[:], bias_gcn3[:], ALU.add).then_inc(s["x1_bias"], 1)
                if st.on(2):
                    pool.wait_ge(s["x2T_mm"], n2)
                    nc.gpsimd.tensor_tensor(x2[:], x2[:], bias_v2[:], ALU.add).then_inc(s["x2_bias"], 1)
                for layer, count in ((3, n3), (2, n2), (0, n0), (1, n1)):
                    if st.on(layer):
                        inv_std(layer, count)

            run_steps(pool, body)

        def blocks_wait(eng, st):
            if isinstance(st.t, int):
                loads = 2 * (min(st.t + 1, PAIRS) + max(0, min(st.t - 1, PAIRS)))
            else:
                loads = 2 * (2 * st.t)
            eng.wait_ge(s["blocks_loaded"], 16 * loads)

        @block.tensor
        def _(pe):
            mm = nc.tensor.matmul

            pe.wait_ge(s_slot[0], 16)
            pe.wait_ge(s_slot[1], 16)
            rq, rk = raw[0], raw[1]
            for c in range(C):
                for o in range(C):
                    last = mm(setup_bank(c), rq[:, o, c * P:(c + 1) * P], rk[:, o, :], start=o == 0, stop=o == C - 1)
                last.then_inc(s_group, 1)
            pe.wait_ge(s_small_ready, 1)
            for o in range(C):
                last = mm(setup_bank(KEY_BIAS), bq_wide[:, o, :], rk[:, o, :], start=o == 0, stop=o == C - 1)
            last.then_inc(s_group, 1)
            for c in range(C):
                for o in range(C):
                    last = mm(setup_bank(ROW_WEIGHTS)[:, c:c + 1], rq[:, o, c * P:(c + 1) * P], bk_col[:, o:o + 1],
                              start=o == 0, stop=o == C - 1)
            last.then_inc(s_group, 1)
            mm(setup_bank(ROW_CONST)[:, 0:1], ones[:], sums[:, 0:1], start=True, stop=True).then_inc(s_group, 1)
            pe.wait_ge(s_qk3_loaded, 16)
            pe.wait_ge(s_edge_used, 1)
            for c in range(C):
                last = nc.tensor.transpose(setup_bank(QK3)[:, c * P:(c + 1) * P], qk3_raw[:, c * P:(c + 1) * P],
                                           ident[:])
            last.then_inc(s_group, 1)

            def end_setup():
                pe.wait_ge(s_group_out, SETUP_GROUPS)
                pe.wait_ge(s_setup_dve, 1)
                pe.wait_ge(s_plain_hi, len(plain))
                pe.wait_ge(s_plain_lo, len(plain) - 1)
                pe.wait_ge(s_pool_lo, 1)
                pe.wait_ge(s_pool_const, 3)

            def turn_v(k):
                _, c = made_v(k)
                slot = k // C
                pe.wait_ge(s_slot[slot], 32)
                pe.wait_ge(s_group_out, SETUP_GROUPS + k - 1)
                b = setup_bank(SETUP_GROUPS + k)
                for o in range(C):
                    last = nc.tensor.transpose(b[:, o * P:(o + 1) * P], raw[slot][:, o, c * P:(c + 1) * P], ident[:])
                last.then_inc(s_group, 1)

            def turn(dst, src):
                for c in range(C):
                    last = nc.tensor.transpose(dst[:, c * P:(c + 1) * P], src[:, c * P:(c + 1) * P], ident[:])
                return last

            def rows_times(dst, xT, w, chunks=range(C), stop=True):
                for c in chunks:
                    for i, (a, b) in enumerate(PASSES):
                        last = mm(dst, xT[:, a, c, :], w[:, b, c, :], start=c == 0 and i == 0,
                                  stop=stop and c == C - 1 and i == 2)
                return last

            def rows_times_part(dst, xT, w, part):
                for c in range(C):
                    for i, (a, b) in enumerate(PASSES):
                        last = mm(dst[:, part], xT[:, a, c, :], w[:, b, c, part], start=c == 0 and i == 0,
                                  stop=c == C - 1 and i == 2)
                return last

            def rows_times_wide(dst, xT, w, lead):
                rows_times_part(dst, xT, w, slice(0, lead))
                return rows_times_part(dst, xT, w, slice(lead, dst.shape[1]))

            def mix(dst, mT, y, start=True, stop=True):
                for i, (a, b) in enumerate(PASSES):
                    last = mm(dst, mT[a], y[:, b], start=start and i == 0, stop=stop and i == 2)
                return last

            def high_low(t):
                return [t[:, H], t[:, L]]

            def support(count, w):
                pe.wait_ge(s["feat_hi"], count)
                pe.wait_ge(s["feat_lo"], count)
                rows_times(gcn_ps, feat1, w).then_inc(s["support_mm"], 1)

            def aggregate(count):
                pe.wait_ge(s["node_hi"], count)
                pe.wait_ge(s["node_lo"], count)
                mix(gcn_ps, [adjT[:, a, 0, :] for a in (H, L)], node1).then_inc(s["gcn_mm"], 1)

            def turn_hidden(count):
                pe.wait_ge(s["hidden1"], count)
                turn(gcn_ps, hidden1).then_inc(s["turn1_mm"], 1)

            def turn_x0(count):
                pe.wait_ge(s["x0_loaded"], 16 * count)
                turn(turn_ps, x0_in).then_inc(s["x0T_mm"], 1)

            def begin_hop1(count):
                pe.wait_ge(s["x0T_hi"], count)
                pe.wait_ge(s["x0T_lo"], count)
                rows_times(hop1_ps, x0T, w_hop1, chunks=range(C - 1), stop=False)

            def body(st):
                zero, one, two, three = (st.on(l) for l in range(LAYERS))
                n0, n1, n2, n3 = (st.now(l) for l in range(LAYERS))
                p0, p1, p2, p3 = (st.before(l) for l in range(LAYERS))

                if zero:
                    rows_times(hop1_ps, x0T, w_hop1, chunks=range(C - 1, C), stop=False)
                if three:
                    pe.wait_ge(s_x[2], n3)
                    wait(pe, s["x0T_lo"], n0)
                    turn(turn_ps, x3).then_inc(s["x3T_mm"], 1)
                if one:
                    pe.wait_ge(s_x[0], n1)
                    wait(pe, s_sum[1], p1)
                    turn(gcn_ps, x0_res).then_inc(s["turn1_mm"], 1)
                if zero:
                    wait(pe, s["adjT_lo"], st.t)
                    wait(pe, s["exp2"], p2)
                    rows_times_wide(wide_a, x0T, w_hop2, LEAD_A).then_inc(s["hop2_mm"], 1)
                if st.is_step(2):
                    pe.wait_ge(s_group_out, ALL_GROUPS)
                if two:
                    pe.wait_ge(s_x[1], n2)
                    wait(pe, s_sum[0], p0)
                    turn(mid_ps, x2).then_inc(s["x2T_mm"], 1)
                if one:
                    support(3 * p1 + 1, w_gcn1)
                if st.is_step(0):
                    end_setup()
                    turn_v(0)
                    turn_v(1)
                if zero:
                    pe.wait_ge(s["diag0"], n0)
                    pe.wait_ge(s["edge_i"], n0)
                    pe.wait_ge(s["y2_lo"], n0)
                    mm(edge_bc_ps, same_graph[:], diag0[:], start=True, stop=True).then_inc(s["edge_bc_mm"], 1)
                if three:
                    pe.wait_ge(s["x3T_hi"], n3)
                    pe.wait_ge(s["x3T_lo"], n3)
                    wait(pe, s_sum[2], p2)
                    rows_times_part(wide_b, x3T, w_v3, slice(LEAD_B, D + 2 * E3)).then_inc(s["qk3_mm"], 1)
                    rows_times_part(wide_b, x3T, w_v3, slice(0, LEAD_B)).then_inc(s["value3_mm"], 1)
                if one:
                    aggregate(3 * p1 + 1)
                if two:
                    pe.wait_ge(s["x2T_hi"], n2)
                    pe.wait_ge(s["x2T_lo"], n2)
                    wait(pe, s["y2_lo"], n0)
                    wait(pe, s["edge_sum"], n0)
                    rows_times_wide(wide_a, x2T, w_qk2, LEAD_A).then_inc(s["query_mm"], 1)
                if one:
                    turn_hidden(2 * p1 + 1)
                if three:
                    pe.wait_ge(s["q3"], n3)
                    pe.wait_ge(s["k3_hi"], n3)
                    pe.wait_ge(s["k3_lo"], n3)
                    mm(nbr3_ps, adjT[:, H, 1, :], k3[:], start=True, stop=False)
                    mm(nbr3_ps[:, 0, :], adjT[:, L, 1, :], k3[:, H], start=False, stop=True).then_inc(s["nbr3_mm"], 1)
                if st.is_step(0):
                    turn_v(2)
                    turn_v(3)
                if zero:
                    pe.wait_ge(s["trans0"], n0)
                    wait(pe, s["x3T_lo"], n3)
                    nc.tensor.transpose(turn_ps[:, 0:P], trans0[:], ident[:]).then_inc(s["trans0T_mm"], 1)
                if two and zero:
                    rows_times(mid_ps, x2T, w_v2).then_inc(s["value_mm"], 1)
                elif two:
                    rows_times(mid_ps, x2T, w_v2, chunks=range(C // 2), stop=False)
                if three:
                    pe.wait_ge(s["diag3"], n3)
                    mm(w3_bc_ps, same_graph[:], diag3[:], start=True, stop=True).then_inc(s["w3_bc_mm"], 1)
                if one:
                    support(3 * p1 + 2, w_gcn2)
                if two:
                    pe.wait_ge(s["query2"], n2)
                    pe.wait_ge(s["rowbias2"], n2)
                    turn(queryT_ps, query2).then_inc(s["queryT_mm"], 1)
                if zero:
                    pe.wait_ge(s["trans0T_hi"], n0)
                    pe.wait_ge(s["trans0T_lo"], n0)
                    pe.wait_ge(s["y2_hi"], n0)
                    mix(hop1_ps, high_low(trans0T), hop_y, start=False).then_inc(s["hop12_mm"], 1)
                if zero:
                    wait(pe, s_sum[0], p0)
                    wait(pe, s["value_hi"], n2)
                    wait(pe, s["value_lo"], n2)
                    rows_times(mid_ps, x0T, w_hop0, chunks=range(1), stop=False)
                if one:
                    aggregate(3 * p1 + 2)
                if two:
                    pe.wait_ge(s["queryT_hi"], n2)
                    pe.wait_ge(s["queryT_lo"], n2)
                    for c in range(C):
                        mm(scores_ps, query2T[:, H, c, :], x2T[:, :, c, :], start=c == 0, stop=False)
                        last = mm(scores_ps[:, 0, :], query2T[:, L, c, :], x2T[:, H, c, :], start=False, stop=c == C - 1)
                    last.then_inc(s["scores_mm"], 1)
                if zero:
                    rows_times(mid_ps, x0T, w_hop0, chunks=range(1, 2), stop=False)
                if st.is_step(0):
                    turn_v(4)
                    turn_v(5)
                if one:
                    turn_hidden(2 * p1 + 2)
                if two and not zero:
                    rows_times(mid_ps, x2T, w_v2, chunks=range(C // 2, C)).then_inc(s["value_mm"], 1)
                if zero:
                    rows_times(mid_ps, x0T, w_hop0, chunks=range(2, C), stop=False).then_inc(s["hop0_mm"], 1)
                if two:
                    pe.wait_ge(s["probs2"], n2)
                    wait(pe, s["trans0T_lo"], n0)
                    wait(pe, s["x3T_lo"], n3)
                    nc.tensor.transpose(turn_ps[:, 0:P], probs2[:], ident[:]).then_inc(s["probs2T_mm"], 1)
                if zero:
                    pe.wait_ge(s["y1_hi"], n0)
                    pe.wait_ge(s["y1_lo"], n0)
                    mix(mid_ps, high_low(trans0T), hop_y, start=False).then_inc(s["hop_mm"], 1)
                if st.blocks_follow():
                    blocks_wait(pe, st)
                    wait(pe, s["queryT_lo"], n2)
                    wait(pe, s["y2_lo"], n0)
                    wait(pe, s["adjT_lo"], st.t)
                    for slot in range(2):
                        last = nc.tensor.transpose(adjT_ps[:, slot * P:(slot + 1) * P], adj_blocks[:, slot, :], ident[:])
                    last.then_inc(s["adjT_mm"], 1)
                if st.pair_follows():
                    wait(pe, s["probs2T_lo"], n2)
                    wait(pe, s["trans0T_lo"], n0)
                    wait(pe, s["x3T_lo"], n3)
                    turn_x0(st.t + 2)
                if two:
                    pe.wait_ge(s["probs2T_hi"], n2)
                    pe.wait_ge(s["probs2T_lo"], n2)
                    pe.wait_ge(s["value_lo"], n2)
                    wait(pe, s_sum[3], n3)
                    wait(pe, s_sum[2], p2)
                    mix(mix_ps, high_low(probs2T), value2).then_inc(s["mix_mm"], 1)
                if one:
                    support(3 * p1 + 3, w_gcn3)
                if st.pair_follows():
                    begin_hop1(st.t + 2)
                if st.is_step(0):
                    turn_v(6)
                    turn_v(7)
                if one:
                    aggregate(3 * p1 + 3)

            pe.wait_ge(s_group_out, 3)
            turn_x0(1)
            pe.wait_ge(s_plain_hi, 1)
            pe.wait_ge(s_plain_lo, 1)
            begin_hop1(1)
            pe.wait_ge(s_group_out, SETUP_GROUPS - 1)
            pe.wait_ge(s_plain_hi, 2)
            pe.wait_ge(s_plain_lo, 2)
            run_steps(pe, body)

        @block.scalar
        def _(act):
            def copy(dst, src):
                return nc.scalar.activation(dst, src, ACT.Copy)

            def chunks(ps):
                return ps.rearrange("p (c n) -> p c n", c=C)

            def turn_x0(count):
                act.wait_ge(s["x0T_mm"], count)
                wait(act, s["hop0_mm"], count - 1)
                copy(x0T[:, H], chunks(turn_ps)).then_inc(s["x0T_hi"], 1)

            def high_plain(i):
                slot, count = PLAIN_SLOT[i]
                act.wait_ge(s_slot[slot], count)
                copy(plain[i][:, H, :, 0:D], raw[slot][:]).then_inc(s_plain_hi, 1)

            def high_m(groups):
                for group in groups:
                    act.wait_ge(s_group, group + 1)
                    copy(w_qk2[:, H, group, 0:D], setup_bank(group)).then_inc(s_group_hi, 1)

            high_plain(0)
            high_m(range(M_GROUPS - 1))
            high_plain(1)
            high_m(range(M_GROUPS - 1, M_GROUPS))
            high_plain(2)
            high_plain(3)
            turn_x0(1)
            act.wait_ge(s_group, QK3 + 1)
            copy(w_v3[:, H, :, D:], setup_bank(QK3).rearrange("p (c n) -> p c n", c=C)).then_inc(s_group_hi, 1)
            for i in range(4, len(plain)):
                high_plain(i)

            def high_v(k):
                if k == 0:
                    act.wait_ge(s_group_out, SETUP_GROUPS)
                act.wait_ge(s_group, SETUP_GROUPS + k + 1)
                w, c = made_v(k)
                copy(w[:, H, c, 0:D], setup_bank(SETUP_GROUPS + k)).then_inc(s_group_hi, 1)

            act.wait_ge(s_setup_dve, 1)
            act.wait_ge(s_pool_lo, 1)

            def high(dst, src, ready, ready_count, done):
                act.wait_ge(ready, ready_count)
                copy(dst, src).then_inc(done, 1)

            def feat_high(count, function=ACT.Relu):
                wait(act, s["support_mm"], count - 1)
                act.wait_ge(s["turn1_mm"], count)
                nc.scalar.activation(feat1[:, H], chunks(gcn_ps), function).then_inc(s["feat_hi"], 1)

            def normalise(l, count):
                act.wait_ge(s_shift[l], count)
                nc.scalar.activation(norm_of[l][:], sum_of[l][:], ACT.Identity, bias=shift[l], scale=rstd[l]) \
                    .then_inc(s_x[l], 1)

            def node_high(count):
                wait(act, s["gcn_mm"], count - 1)
                high(node1[:, H], gcn_ps, s["support_mm"], count, s["node_hi"])

            def body(st):
                zero, one, two, three = (st.on(l) for l in range(LAYERS))
                n0, n1, n2, n3 = (st.now(l) for l in range(LAYERS))
                p0, p1, p2, p3 = (st.before(l) for l in range(LAYERS))

                def high_value():
                    wait(act, s["mix_mm"], p2)
                    high(value2[:, H], mid_ps, s["value_mm"], n2, s["value_hi"])

                def high_query():
                    wait(act, s["value3_mm"], n3)
                    high(query2T[:, H], chunks(queryT_ps), s["queryT_mm"], n2, s["queryT_hi"])

                if three:
                    wait(act, s["scores_mm"], p2)
                    high(x3T[:, H], chunks(turn_ps), s["x3T_mm"], n3, s["x3T_hi"])
                if one:
                    feat_high(3 * p1 + 1, ACT.Copy)
                if zero:
                    wait(act, s["hop_mm"], p0)
                    high(hop_y[:, H], wide_a[:, 0:D], s["hop2_mm"], n0, s["y2_hi"])
                if two:
                    wait(act, s["scores_mm"], p2)
                    high(x2T[:, H], chunks(mid_ps), s["x2T_mm"], n2, s["x2T_hi"])
                if one:
                    node_high(3 * p1 + 1)
                if st.is_step(0):
                    high_v(0)
                    high_v(1)
                if zero:
                    act.wait_ge(s["edge_lrelu"], n0)
                    nc.scalar.activation(edge0[:], edge0[:], ACT.Exp).then_inc(s["edge_exp"], 1)
                if three:
                    wait(act, s["w3"], p3)
                    act.wait_ge(s["qk3_mm"], n3)
                    copy(q3[:], wide_b[:, D:D + E3]).then_inc(s["q3"], 1)
                    wait(act, s["nbr3_mm"], p3)
                    copy(k3[:, H], wide_b[:, D + E3:]).then_inc(s["k3_hi"], 1)
                if one:
                    feat_high(3 * p1 + 2)
                if st.is_step(0):
                    high_v(2)
                    high_v(3)
                if zero:
                    wait(act, s["hop_mm"], p0)
                    high(trans0T[:, H], turn_ps[:, 0:P], s["trans0T_mm"], n0, s["trans0T_hi"])
                if two and zero:
                    high_value()
                if two and not one:
                    high_query()
                if three:
                    act.wait_ge(s["neg3"], n3)
                    nc.scalar.activation(work3[:, 0, :], w3_bc_ps, ACT.Exp, bias=max3,
                                         accum_out=sum3).then_inc(s["exp3_all"], 1)
                    nc.scalar.activation(exp3, w3, ACT.Exp, bias=max3).then_inc(s["exp3"], 1)
                if one:
                    node_high(3 * p1 + 2)
                if two and one:
                    high_query()
                if zero:
                    high(hop_y[:, H], hop1_ps, s["hop12_mm"], n0, s["y1_hi"])
                if st.is_step(0):
                    high_v(4)
                    high_v(5)
                if two:
                    act.wait_ge(s["scores2"], n2)
                    nc.scalar.activation(attn2[:], attn2[:], ACT.Exp, bias=rowbias2).then_inc(s["exp2"], 1)
                if one:
                    feat_high(3 * p1 + 3)
                if two and not zero:
                    high_value()
                if two:
                    wait(act, s["mix_mm"], p2)
                    high(probs2T[:, H], turn_ps[:, 0:P], s["probs2T_mm"], n2, s["probs2T_hi"])
                if st.pair_follows():
                    turn_x0(st.t + 2)
                if one:
                    node_high(3 * p1 + 3)
                if st.is_step(0):
                    high_v(6)
                    high_v(7)
                if three:
                    if st.pair_follows():
                        act.wait_ge(s["x0T_mm"], st.t + 2)
                    wait(act, s["out_stored"], 16 * p3)
                    normalise(3, n3)
                if zero:
                    normalise(0, n0)
                if st.blocks_follow():
                    wait(act, s["gcn_mm"], 3 * n1)
                    wait(act, s["nbr3_mm"], n3)
                    act.wait_ge(s["adjT_mm"], st.t + 1)
                    copy(adjT[:, H], adjT_ps.rearrange("p (a n) -> p a n", a=2)).then_inc(s["adjT_hi"], 1)

            run_steps(act, body)

        @block.vector
        def _(dve):
            setup_step = [0]

            def link(ins):
                setup_step[0] += 1
                ins.then_inc(s_dve_setup, 1)
                dve.wait_ge(s_dve_setup, setup_step[0])

            ve = nc.vector
            ve.memset(ones[:], 1.0)
            ve.memset(same_graph[:], 0.0)
            link(ve.memset(row_raw[:], 0.0))
            for g in HALVES:
                ve.memset(same_graph[g, g], 1.0)
            dve.wait_ge(s_vec_loaded, 16 * VECTORS)
            dve.wait_ge(s_pool_const, 2)
            for c in range(C):
                ve.tensor_scalar(bq_wide[:, c, :], ones[:], bq_col[:, c:c + 1], None, ALU.mult)
            link(ve.tensor_tensor_reduce(out=junk[:, 0:C], in0=bq_col[:], in1=bk_col[:], scale=1.0, scalar=0.0,
                                         op0=ALU.mult, op1=ALU.add, accum_out=sums[:, 0:1]))
            ve.tensor_tensor(node_ident[:], ident[:, 0:N], ident[:, N:P], ALU.add).then_inc(s_small_ready, 1)
            for a in range(2):
                last = ve.tensor_tensor_reduce(out=junk, in0=bv_all[:, 0, :], in1=aw_all[:, a, :], scale=1.0, scalar=0.0,
                                               op0=ALU.mult, op1=ALU.add, accum_out=sums[:, 1 + a:2 + a])
                link(last)
            dve.wait_ge(s_slot[2], 16)
            for c in range(C):
                for a in range(2):
                    link(ve.tensor_tensor_reduce(out=junk, in0=raw[2][:, c, :], in1=aw_all[:, a, :], scale=1.0,
                                                 scalar=0.0, op0=ALU.mult, op1=ALU.add,
                                                 accum_out=edge_raw[:, c, a:a + 1]))
            link(ve.tensor_copy(w_hop2[:, H, :, D:], edge_raw[:]))
            ve.tensor_tensor(w_hop2[:, L, :, D:], edge_raw[:], w_hop2[:, H, :, D:].bitcast(F32), ALU.subtract) \
                .then_inc(s_edge_used, 1)
            link(ve.tensor_tensor(edge_const, sums[:, 1:2], sums[:, 2:3], ALU.add))
            link(ve.tensor_tensor(edge_const, edge_const, ab_all[:], ALU.add))
            dve.wait_ge(s_bias_loaded, 16 * BIASES)
            for b in bias_hops:
                link(ve.tensor_tensor(bias_hop[:], bias_hop[:], b[:, 0, :], ALU.add))
            def chunks(ps):
                return ps.rearrange("p (c n) -> p c n", c=C)

            def low(dst, src, high, hi_done, hi_count, done):
                dve.wait_ge(hi_done, hi_count)
                ve.tensor_tensor(dst, src, high.bitcast(F32), ALU.subtract).then_inc(done, 1)

            def turn_x0(count):
                wait(dve, s["hop0_mm"], count - 1)
                low(x0T[:, L], chunks(turn_ps), x0T[:, H], s["x0T_hi"], count, s["x0T_lo"])

            def low_plain(i):
                dve.wait_ge(s_plain_hi, i + 1)
                slot = PLAIN_SLOT[i][0]
                ve.tensor_tensor(plain[i][:, L, :, 0:D], raw[slot][:], plain[i][:, H, :, 0:D].bitcast(F32),
                                 ALU.subtract).then_inc(s_plain_lo, 1)

            def low_m(groups):
                for group in groups:
                    dve.wait_ge(s_group_hi, group + 1)
                    ve.tensor_tensor(w_qk2[:, L, group, 0:D], setup_bank(group), w_qk2[:, H, group, 0:D].bitcast(F32),
                                     ALU.subtract).then_inc(s_group_out, 1)

            low_plain(0)
            low_m(range(M_GROUPS - 1))
            low_plain(1)
            low_m(range(M_GROUPS - 1, M_GROUPS))
            low_plain(2)
            dve.wait_ge(s_group, KEY_BIAS + 1)
            ve.tensor_copy(bias_key2[:], setup_bank(KEY_BIAS)).then_inc(s_group_out, 1)
            dve.wait_ge(s_group, ROW_WEIGHTS + 1)
            link(ve.tensor_copy(row_raw[:, :, 0:1], setup_bank(ROW_WEIGHTS)[:, 0:C].rearrange("p (c a) -> p c a", a=1)))
            link(ve.tensor_copy(w_qk2[:, H, :, D:], row_raw[:]))
            ve.tensor_tensor(w_qk2[:, L, :, D:], row_raw[:], w_qk2[:, H, :, D:].bitcast(F32), ALU.subtract) \
                .then_inc(s_group_out, 1)
            dve.wait_ge(s_group, ROW_CONST + 1)
            ve.tensor_copy(row_const, setup_bank(ROW_CONST)[:, 0:1]).then_inc(s_group_out, 1)
            turn_x0(1)
            dve.wait_ge(s_group_hi, M_GROUPS + 1)
            ve.tensor_tensor(w_v3[:, L, :, D:], setup_bank(QK3).rearrange("p (c n) -> p c n", c=C),
                             w_v3[:, H, :, D:].bitcast(F32), ALU.subtract).then_inc(s_group_out, 1)
            for i in range(3, len(plain)):
                if i != ON_POOL:
                    low_plain(i)
            dve.wait_ge(s_plain_lo, len(plain) - 1)
            dve.wait_ge(s_group_out, SETUP_GROUPS)
            ve.memset(pad, 0.0).then_inc(s_setup_dve, 1)

            def low_v(k):
                dve.wait_ge(s_group_hi, M_GROUPS + 1 + k + 1)
                w, c = made_v(k)
                ve.tensor_tensor(w[:, L, c, 0:D], setup_bank(SETUP_GROUPS + k), w[:, H, c, 0:D].bitcast(F32),
                                 ALU.subtract).then_inc(s_group_out, 1)

            dve.wait_ge(s_pool_lo, 1)

            def feat_low(count):
                dve.wait_ge(s["feat_hi"], count)
                ve.scalar_tensor_tensor(out=feat1[:, L], in0=chunks(gcn_ps), scalar=0.0, in1=feat1[:, H].bitcast(F32),
                                        op0=ALU.max, op1=ALU.subtract).then_inc(s["feat_lo"], 1)

            def hidden(gcn_count, bias, query_count):
                dve.wait_ge(s["gcn_mm"], gcn_count)
                wait(dve, s["turn1_mm"], gcn_count)
                wait(dve, s["queryT_mm"], query_count)
                ve.tensor_tensor(hidden1[:], gcn_ps, bias[:], ALU.add).then_inc(s["hidden1"], 1)

            def node_low(count):
                low(node1[:, L], gcn_ps, node1[:, H], s["node_hi"], count, s["node_lo"])

            def diagonal_blocks(dst, src, scale, done):
                for g in HALVES:
                    last = ve.tensor_scalar(dst[g, g], src[g, :], scale[g, :], None, ALU.mult)
                last.then_inc(done, 1)

            def statistics(l, count):
                dve.wait_ge(s_sum[l], count)
                ve.bn_stats(stats[l], sum_of[l][:]).then_inc(s_stats[l], 1)

            def moments_of(l):
                ve.bn_aggr(moments[l], stats[l]).then_inc(s_moments[l], 1)

            def add_eps(l, count):
                dve.wait_ge(s_moments[l], count)
                ve.tensor_scalar(var_eps[l], moments[l][:, 1:2], LN_EPS, None, ALU.add).then_inc(s_vareps[l], 1)

            def normalise(l, count):
                dve.wait_ge(s_rstd[l], count)
                ve.tensor_scalar(norm_of[l][:], sum_of[l][:], moments[l][:, 0:1], rstd[l], ALU.subtract, ALU.mult) \
                    .then_inc(s_x[l], 1)

            def shift_of(l, count):
                dve.wait_ge(s_rstd[l], count)
                ve.scalar_tensor_tensor(out=shift[l], in0=moments[l][:, 0:1], scalar=-1.0, in1=rstd[l],
                                        op0=ALU.mult, op1=ALU.mult).then_inc(s_shift[l], 1)

            def body(st):
                zero, one, two, three = (st.on(l) for l in range(LAYERS))
                n0, n1, n2, n3 = (st.now(l) for l in range(LAYERS))
                p0, p1, p2, p3 = (st.before(l) for l in range(LAYERS))

                def low_value():
                    low(value2[:, L], mid_ps, value2[:, H], s["value_hi"], n2, s["value_lo"])

                def low_query():
                    low(query2T[:, L], chunks(queryT_ps), query2T[:, H], s["queryT_hi"], n2, s["queryT_lo"])

                if one:
                    low(feat1[:, L], chunks(gcn_ps), feat1[:, H], s["feat_hi"], 3 * p1 + 1, s["feat_lo"])
                if three:
                    low(x3T[:, L], chunks(turn_ps), x3T[:, H], s["x3T_hi"], n3, s["x3T_lo"])
                if zero:
                    low(hop_y[:, L], wide_a[:, 0:D], hop_y[:, H], s["y2_hi"], n0, s["y2_lo"])
                    wait(dve, s["edge_bc_mm"], p0)
                    wait(dve, s["w3_bc_mm"], p3)
                    ve.tensor_scalar(diag0[:], node_ident[:], wide_a[:, D:D + 1], None, ALU.mult) \
                        .then_inc(s["diag0"], 1)
                    ve.tensor_tensor(edge_i, wide_a[:, D + 1:D + 2], edge_const, ALU.add).then_inc(s["edge_i"], 1)
                if two:
                    low(x2T[:, L], chunks(mid_ps), x2T[:, H], s["x2T_hi"], n2, s["x2T_lo"])
                if one:
                    node_low(3 * p1 + 1)
                if st.is_step(0):
                    low_v(0)
                    low_v(1)
                if zero:
                    dve.wait_ge(s["edge_bc_mm"], n0)
                    dve.wait_ge(s["edge_i"], n0)
                    wait(dve, s["exp3_all"], p3)
                    ve.tensor_scalar(edge0[:], edge_bc_ps, edge_i, None, ALU.add).then_inc(s["edge_sum"], 1)
                    dve.wait_ge(s["edge_sum"], n0)
                    ve.scalar_tensor_tensor(out=edge0[:], in0=edge0[:], scalar=SLOPE, in1=edge0[:], op0=ALU.mult,
                                            op1=ALU.max).then_inc(s["edge_lrelu"], 1)
                    dve.wait_ge(s["edge_exp"], n0)
                    dve.wait_ge(s["adj0_loaded"], 16 * n0)
                    ve.tensor_tensor_reduce(out=edge0[:], in0=edge0[:], in1=adj0[:], scale=1.0, scalar=0.0,
                                            op0=ALU.mult, op1=ALU.add, accum_out=rowsum0).then_inc(s["alpha0"], 1)
                    dve.wait_ge(s["alpha0"], n0)
                    ve.tensor_scalar(rowsum0, rowsum0, ROWSUM_EPS, None, ALU.add).then_inc(s["den0"], 1)
                    dve.wait_ge(s["den0"], n0)
                    ve.reciprocal(inv0, rowsum0).then_inc(s["inv0"], 1)
                    dve.wait_ge(s["inv0"], n0)
                    wait(dve, s["trans0T_mm"], p0)
                    diagonal_blocks(trans0, edge0, inv0, s["trans0"])
                if three:
                    low(k3[:, L], wide_b[:, D + E3:], k3[:, H], s["k3_hi"], n3, s["k3_lo"])
                if one:
                    dve.wait_ge(s["x1_bias"], n1)
                    hidden(3 * p1 + 1, bias_gcn1, p2)
                if two:
                    dve.wait_ge(s["query_mm"], n2)
                    wait(dve, s["exp2"], p2)
                    ve.tensor_tensor(rowbias2, wide_a[:, D:D + 1], row_const, ALU.add).then_inc(s["rowbias2"], 1)
                if one:
                    feat_low(3 * p1 + 2)
                if three:
                    dve.wait_ge(s["nbr3_mm"], n3)
                    dve.wait_ge(s["q3"], n3)
                    wait(dve, s["trans0"], n0)
                    wait(dve, s["exp3_all"], p3)
                    wait(dve, s["exp3"], p3)
                    wait(dve, s["w3_bc_mm"], p3)
                    wait(dve, s["edge_bc_mm"], n0)
                    q_twice = q3[:].rearrange("p (a n) -> p a n", a=1).broadcast_to([P, 2, E3])
                    ve.tensor_tensor_reduce(out=work3[:], in0=q_twice, in1=nbr3_ps, scale=SCALE3, scalar=0.0,
                                            op0=ALU.mult, op1=ALU.add, accum_out=w3).then_inc(s["w3"], 1)
                    dve.wait_ge(s["w3"], n3)
                    ve.tensor_scalar(diag3[:], node_ident[:], w3, None, ALU.mult).then_inc(s["diag3"], 1)
                if st.is_step(0):
                    low_v(2)
                    low_v(3)
                if zero:
                    low(trans0T[:, L], turn_ps[:, 0:P], trans0T[:, H], s["trans0T_hi"], n0, s["trans0T_lo"])
                if two:
                    wait(dve, s["turn1_mm"], 3 * p1 + 2 if one else 3 * n1)
                    ve.tensor_tensor(query2[:], wide_a[:, 0:D], bias_key2[:], ALU.add).then_inc(s["query2"], 1)
                if two and zero:
                    low_value()
                if two and not one:
                    low_query()
                if three:
                    dve.wait_ge(s["w3_bc_mm"], n3)
                    ve.reduce_max(max3, w3_bc_ps, AX.X).then_inc(s["max3"], 1)
                    dve.wait_ge(s["max3"], n3)
                    ve.tensor_scalar(max3, max3, -1.0, None, ALU.mult).then_inc(s["neg3"], 1)
                if three:
                    dve.wait_ge(s["exp3_all"], n3)
                    ve.reciprocal(inv3, sum3).then_inc(s["inv3"], 1)
                    dve.wait_ge(s["inv3"], n3)
                    dve.wait_ge(s["exp3"], n3)
                    ve.tensor_tensor(gate3, exp3, inv3, ALU.mult).then_inc(s["gate3"], 1)
                if three:
                    dve.wait_ge(s["gate3"], n3)
                    dve.wait_ge(s["value3_mm"], n3)
                    ve.scalar_tensor_tensor(out=x3[:], in0=wide_b[:, 0:D], scalar=gate3, in1=x3[:], op0=ALU.mult,
                                            op1=ALU.add).then_inc(s_sum[3], 1)
                if one:
                    node_low(3 * p1 + 2)
                if two and one:
                    low_query()
                if one:
                    hidden(3 * p1 + 2, bias_gcn2, n2)
                if two:
                    dve.wait_ge(s["scores_mm"], n2)
                    wait(dve, s["probs2"], p2)
                    for g in HALVES:
                        last = ve.tensor_reduce(attn2[g, :], scores_ps[g, :, g].rearrange("p a n -> p n a"), AX.X, ALU.add)
                    last.then_inc(s["scores2"], 1)
                if st.is_step(0):
                    low_v(4)
                    low_v(5)
                if zero:
                    low(hop_y[:, L], hop1_ps, hop_y[:, H], s["y1_hi"], n0, s["y1_lo"])
                if two:
                    dve.wait_ge(s["exp2"], n2)
                    dve.wait_ge(s["adj2_loaded"], 16 * n2)
                    ve.tensor_tensor_reduce(out=attn2[:], in0=attn2[:], in1=adj2[:], scale=1.0, scalar=0.0,
                                            op0=ALU.mult, op1=ALU.add, accum_out=rowsum2).then_inc(s["attn2"], 1)
                    dve.wait_ge(s["attn2"], n2)
                    ve.reciprocal(inv2, rowsum2).then_inc(s["inv2"], 1)
                    dve.wait_ge(s["inv2"], n2)
                    wait(dve, s["probs2T_mm"], p2)
                    diagonal_blocks(probs2, attn2, inv2, s["probs2"])
                if two and not zero:
                    low_value()
                if three:
                    statistics(3, n3)
                if two:
                    low(probs2T[:, L], turn_ps[:, 0:P], probs2T[:, H], s["probs2T_hi"], n2, s["probs2T_lo"])
                if one:
                    feat_low(3 * p1 + 3)
                if zero:
                    dve.wait_ge(s["hop_mm"], n0)
                    ve.tensor_tensor(mid_ps, mid_ps, bias_hop[:], ALU.add).then_inc(s["hop_bias"], 1)
                if three:
                    dve.wait_ge(s_stats[3], n3)
                    ve.memset(pad, 0.0)
                    moments_of(3)
                    add_eps(3, n3)
                if st.pair_follows():
                    turn_x0(st.t + 2)
                if two:
                    dve.wait_ge(s["mix_mm"], n2)
                    dve.wait_ge(s["x2_bias"], n2)
                    ve.tensor_tensor(x2[:], mix_ps, x2[:], ALU.add).then_inc(s_sum[2], 1)
                if zero:
                    dve.wait_ge(s["hop_bias"], n0)
                    dve.wait_ge(s["res_loaded"], 16 * n0)
                    ve.scalar_tensor_tensor(out=x0_res[:], in0=mid_ps, scalar=0.0, in1=x0_res[:], op0=ALU.max,
                                            op1=ALU.add).then_inc(s_sum[0], 1)
                if two:
                    statistics(2, n2)
                if three:
                    shift_of(3, n3)
                if zero:
                    statistics(0, n0)
                if two:
                    dve.wait_ge(s_stats[2], n2)
                    ve.memset(pad, 0.0)
                    moments_of(2)
                if zero:
                    dve.wait_ge(s_stats[0], n0)
                    ve.memset(pad0, 0.0)
                    moments_of(0)
                if two:
                    add_eps(2, n2)
                if zero:
                    add_eps(0, n0)
                if one:
                    node_low(3 * p1 + 3)
                if st.is_step(0):
                    low_v(6)
                    low_v(7)
                if two:
                    wait(dve, s_x[3], n3)
                    normalise(2, n2)
                if zero:
                    shift_of(0, n0)
                if one:
                    dve.wait_ge(s["gcn_mm"], 3 * n1)
                    dve.wait_ge(s["x1_bias"], n1)
                    ve.tensor_tensor(x1[:], gcn_ps, x1[:], ALU.add).then_inc(s_sum[1], 1)
                if st.blocks_follow():
                    low(adjT[:, L], adjT_ps.rearrange("p (a n) -> p a n", a=2), adjT[:, H],
                        s["adjT_hi"], st.t + 1, s["adjT_lo"])
                if one:
                    statistics(1, n1)
                    dve.wait_ge(s_stats[1], n1)
                    ve.memset(pad, 0.0)
                    moments_of(1)
                    add_eps(1, n1)
                    wait(dve, s_x[2], n2)
                    normalise(1, n1)

            run_steps(dve, body)


_INS = ['x', 'adj', 'L0_gnn_Wv', 'L0_gnn_bv', 'L0_gnn_aw', 'L0_gnn_ab', 'L0_gnn_Wk', 'L0_gnn_bk',
        'L1_gnn_W1', 'L1_gnn_b1', 'L1_gnn_W2', 'L1_gnn_b2', 'L1_gnn_W3', 'L1_gnn_b3',
        'L2_gnn_Wq_w', 'L2_gnn_Wq_b', 'L2_gnn_Wk_w', 'L2_gnn_Wk_b', 'L2_gnn_Wv_w', 'L2_gnn_Wv_b',
        'L3_gnn_W_qk', 'L3_gnn_W_v']


def kernel(**inputs):
    import numpy as _np
    import concourse.bacc as _bacc
    from concourse import mybir as _mybir
    from concourse.bass_utils import run_bass_kernel_spmd as _run

    nc = _bacc.Bacc("TRN2", target_bir_lowering=False, num_devices=1)
    arrays, args = {}, []
    for name in _INS:
        a = _np.ascontiguousarray(inputs[name])
        arrays[f"in_{name}_dram"] = a
        args.append(nc.dram_tensor(f"in_{name}_dram", a.shape, _mybir.dt.from_np(a.dtype), kind="ExternalInput").ap())
    args.append(nc.dram_tensor("out_0_dram", inputs["x"].shape, _mybir.dt.float32, kind="ExternalOutput").ap())
    build(nc, *args)
    r = _run(nc, [arrays], core_ids=[0])
    return r.results[0]["out_0_dram"]
```
